# Optimizing a Trainium2 kernel written in Bass

```python
import numpy as np
import jax
import jax.numpy as jnp

def _softmax(x, axis=-1):
    return jax.nn.softmax(x, axis=axis)

def _gelu(x):
    return jax.nn.gelu(x, approximate=True)

def _silu(x):
    return jax.nn.silu(x)

def _sigmoid(x):
    return jax.nn.sigmoid(x)

def _layernorm(x, axis=-1, eps=1e-05):
    m = jnp.mean(x, axis=axis, keepdims=True)
    v = jnp.var(x, axis=axis, keepdims=True)
    return (x - m) / jnp.sqrt(v + eps)

def _scatter_add(tgt, idx, src, axis=0):
    return tgt.at[idx].add(src)

def _segment_sum(src, seg, n):
    return jax.ops.segment_sum(src, seg, n)
kernel_name = 'mk_dlrm_tower_d1_rec_r8_7ed6f2'

def setup_inputs(seed: int=0):
    np.random.seed(seed)
    _w = jnp.asarray

    def _rec_inputs():
        import jax
        import jax.numpy as jnp
        _tk = jax.random.key(seed)
        ids = jnp.stack([jax.random.randint(jax.random.fold_in(_tk, 200 + f), (2048,), 0, v, jnp.int32) for f, v in enumerate([1250, 1250, 1000, 1250, 125000, 12500, 1000, 1000, 1250, 1250, 12500, 12500, 1250, 1000, 1250, 12500, 1000, 12500, 1000, 1250, 12500, 12500, 12500, 1250, 1000, 1250])], axis=1)
        tbl_0 = 0.05 * jax.random.normal(jax.random.fold_in(_tk, 500 + 0), (1250, 128), jnp.float32)
        tbl_1 = 0.05 * jax.random.normal(jax.random.fold_in(_tk, 500 + 1), (1250, 128), jnp.float32)
        tbl_2 = 0.05 * jax.random.normal(jax.random.fold_in(_tk, 500 + 2), (1000, 128), jnp.float32)
        tbl_3 = 0.05 * jax.random.normal(jax.random.fold_in(_tk, 500 + 3), (1250, 128), jnp.float32)
        tbl_4 = 0.05 * jax.random.normal(jax.random.fold_in(_tk, 500 + 4), (125000, 128), jnp.float32)
        tbl_5 = 0.05 * jax.random.normal(jax.random.fold_in(_tk, 500 + 5), (12500, 128), jnp.float32)
        tbl_6 = 0.05 * jax.random.normal(jax.random.fold_in(_tk, 500 + 6), (1000, 128), jnp.float32)
        tbl_7 = 0.05 * jax.random.normal(jax.random.fold_in(_tk, 500 + 7), (1000, 128), jnp.float32)
        tbl_8 = 0.05 * jax.random.normal(jax.random.fold_in(_tk, 500 + 8), (1250, 128), jnp.float32)
        tbl_9 = 0.05 * jax.random.normal(jax.random.fold_in(_tk, 500 + 9), (1250, 128), jnp.float32)
        tbl_10 = 0.05 * jax.random.normal(jax.random.fold_in(_tk, 500 + 10), (12500, 128), jnp.float32)
        tbl_11 = 0.05 * jax.random.normal(jax.random.fold_in(_tk, 500 + 11), (12500, 128), jnp.float32)
        tbl_12 = 0.05 * jax.random.normal(jax.random.fold_in(_tk, 500 + 12), (1250, 128), jnp.float32)
        tbl_13 = 0.05 * jax.random.normal(jax.random.fold_in(_tk, 500 + 13), (1000, 128), jnp.float32)
        tbl_14 = 0.05 * jax.random.normal(jax.random.fold_in(_tk, 500 + 14), (1250, 128), jnp.float32)
        tbl_15 = 0.05 * jax.random.normal(jax.random.fold_in(_tk, 500 + 15), (12500, 128), jnp.float32)
        tbl_16 = 0.05 * jax.random.normal(jax.random.fold_in(_tk, 500 + 16), (1000, 128), jnp.float32)
        tbl_17 = 0.05 * jax.random.normal(jax.random.fold_in(_tk, 500 + 17), (12500, 128), jnp.float32)
        tbl_18 = 0.05 * jax.random.normal(jax.random.fold_in(_tk, 500 + 18), (1000, 128), jnp.float32)
        tbl_19 = 0.05 * jax.random.normal(jax.random.fold_in(_tk, 500 + 19), (1250, 128), jnp.float32)
        tbl_20 = 0.05 * jax.random.normal(jax.random.fold_in(_tk, 500 + 20), (12500, 128), jnp.float32)
        tbl_21 = 0.05 * jax.random.normal(jax.random.fold_in(_tk, 500 + 21), (12500, 128), jnp.float32)
        tbl_22 = 0.05 * jax.random.normal(jax.random.fold_in(_tk, 500 + 22), (12500, 128), jnp.float32)
        tbl_23 = 0.05 * jax.random.normal(jax.random.fold_in(_tk, 500 + 23), (1250, 128), jnp.float32)
        tbl_24 = 0.05 * jax.random.normal(jax.random.fold_in(_tk, 500 + 24), (1000, 128), jnp.float32)
        tbl_25 = 0.05 * jax.random.normal(jax.random.fold_in(_tk, 500 + 25), (1250, 128), jnp.float32)
        _rk = jax.random.fold_in(_tk, 7)
        r_dense_features = -0.000520686 + 1.00062 * jax.random.normal(jax.random.fold_in(_rk, 101), (2048, 128), jnp.float32)
        W_top1 = 0.0405887 * jax.random.normal(jax.random.fold_in(_tk, 801), (607, 512), jnp.float32)
        W_top2 = 0.0441942 * jax.random.normal(jax.random.fold_in(_tk, 802), (512, 256), jnp.float32)
        W_top3 = 0.0625 * jax.random.normal(jax.random.fold_in(_tk, 803), (256, 1), jnp.float32)
        b_top1 = jnp.zeros((512,), jnp.float32)
        b_top2 = jnp.zeros((256,), jnp.float32)
        return (r_dense_features, ids, tbl_0, tbl_1, tbl_2, tbl_3, tbl_4, tbl_5, tbl_6, tbl_7, tbl_8, tbl_9, tbl_10, tbl_11, tbl_12, tbl_13, tbl_14, tbl_15, tbl_16, tbl_17, tbl_18, tbl_19, tbl_20, tbl_21, tbl_22, tbl_23, tbl_24, tbl_25, W_top1, b_top1, W_top2, b_top2, W_top3)
    r_dense_features, ids, tbl_0, tbl_1, tbl_2, tbl_3, tbl_4, tbl_5, tbl_6, tbl_7, tbl_8, tbl_9, tbl_10, tbl_11, tbl_12, tbl_13, tbl_14, tbl_15, tbl_16, tbl_17, tbl_18, tbl_19, tbl_20, tbl_21, tbl_22, tbl_23, tbl_24, tbl_25, W_top1, b_top1, W_top2, b_top2, W_top3 = _rec_inputs()

    def _L0_rec_setup():
        import jax, jax.numpy as jnp
        import numpy as np
        NUM_SPARSE = 26
        EMBED_DIM = 128
        BATCH = 2048
        key = jax.random.key(seed)
        k1, k2 = jax.random.split(key)
        dense_features = jax.random.normal(k1, (BATCH, EMBED_DIM), dtype=jnp.float32)
        sparse_features = jax.random.normal(k2, (BATCH, NUM_SPARSE, EMBED_DIM), dtype=jnp.float32)
        return {'dense_features': dense_features, 'sparse_features': sparse_features}
    _L0_rec_all = _L0_rec_setup()
    _L0_rec_in = {k: v for k, v in _L0_rec_all.items() if k in ()}
    del _L0_rec_all
    return {'r_dense_features': r_dense_features, 'ids': ids, 'tbl_0': tbl_0, 'tbl_1': tbl_1, 'tbl_2': tbl_2, 'tbl_3': tbl_3, 'tbl_4': tbl_4, 'tbl_5': tbl_5, 'tbl_6': tbl_6, 'tbl_7': tbl_7, 'tbl_8': tbl_8, 'tbl_9': tbl_9, 'tbl_10': tbl_10, 'tbl_11': tbl_11, 'tbl_12': tbl_12, 'tbl_13': tbl_13, 'tbl_14': tbl_14, 'tbl_15': tbl_15, 'tbl_16': tbl_16, 'tbl_17': tbl_17, 'tbl_18': tbl_18, 'tbl_19': tbl_19, 'tbl_20': tbl_20, 'tbl_21': tbl_21, 'tbl_22': tbl_22, 'tbl_23': tbl_23, 'tbl_24': tbl_24, 'tbl_25': tbl_25, 'W_top1': W_top1, 'b_top1': b_top1, 'W_top2': W_top2, 'b_top2': b_top2, 'W_top3': W_top3}

def reference(r_dense_features, ids, tbl_0, tbl_1, tbl_2, tbl_3, tbl_4, tbl_5, tbl_6, tbl_7, tbl_8, tbl_9, tbl_10, tbl_11, tbl_12, tbl_13, tbl_14, tbl_15, tbl_16, tbl_17, tbl_18, tbl_19, tbl_20, tbl_21, tbl_22, tbl_23, tbl_24, tbl_25, W_top1, b_top1, W_top2, b_top2, W_top3):
    import jax
    import jax.numpy as jnp

    def _L0_rec_ref(dense_features, sparse_features):
        import jax, jax.numpy as jnp
        import numpy as np
        NUM_SPARSE = 26
        EMBED_DIM = 128
        BATCH = 2048
        F = NUM_SPARSE + 1
        combined = jnp.concatenate([dense_features[:, None, :], sparse_features], axis=1)
        interactions = jnp.einsum('bfd,bgd->bfg', combined, combined)
        iu, ju = jnp.triu_indices(F, k=1)
        interactions_flat = interactions[:, iu, ju]
        return jnp.concatenate([dense_features, interactions_flat], axis=1)
    e = jnp.stack([tbl_0[ids[:, 0]], tbl_1[ids[:, 1]], tbl_2[ids[:, 2]], tbl_3[ids[:, 3]], tbl_4[ids[:, 4]], tbl_5[ids[:, 5]], tbl_6[ids[:, 6]], tbl_7[ids[:, 7]], tbl_8[ids[:, 8]], tbl_9[ids[:, 9]], tbl_10[ids[:, 10]], tbl_11[ids[:, 11]], tbl_12[ids[:, 12]], tbl_13[ids[:, 13]], tbl_14[ids[:, 14]], tbl_15[ids[:, 15]], tbl_16[ids[:, 16]], tbl_17[ids[:, 17]], tbl_18[ids[:, 18]], tbl_19[ids[:, 19]], tbl_20[ids[:, 20]], tbl_21[ids[:, 21]], tbl_22[ids[:, 22]], tbl_23[ids[:, 23]], tbl_24[ids[:, 24]], tbl_25[ids[:, 25]]], axis=1)
    z = _L0_rec_ref(r_dense_features, e)
    z = z.reshape(z.shape[0], -1)
    h = jnp.concatenate([z, r_dense_features], axis=1)
    h = jnp.maximum(h @ W_top1 + b_top1, 0.0)
    h = jnp.maximum(h @ W_top2 + b_top2, 0.0)
    y = h @ W_top3
    return y

_drawn_inputs = setup_inputs


def setup_inputs(seed=0):
    import zlib

    import numpy as np

    out = dict(_drawn_inputs(seed))
    spreads = {'b_top1': (0.0, 0.1), 'b_top2': (0.0, 0.1)}
    factors = {}
    for name, (base, spread) in spreads.items():
        noise = np.random.default_rng([zlib.crc32(name.encode()), seed]).standard_normal(out[name].shape)
        drawn = base * np.exp(spread * noise) if base else spread * noise
        out[name] = jnp.asarray(drawn.astype(out[name].dtype))
    for name, factor in factors.items():
        out[name] = (out[name] * factor).astype(out[name].dtype)
    return out
```

```python
import concourse.bass as bass
from concourse import mybir
from contextlib import ExitStack

P = 128
BATCH = 2048
DIM = 128
FEATS = 27
SLOTS = 32
TILE = 128
TILES = 4
BLOCK = 2 * TILE
PAIR_ROWS = FEATS * (FEATS - 1) // 2
TURNS = BATCH // (TILES * TILE)
HID1, HID2 = 512, 256

SMALL = [2, 6, 7, 13, 16, 18, 24]
LARGE = [f for f in range(FEATS - 1) if f not in SMALL]
SMALL_ROWS = 1000
CHUNKS = 8
ROWS_P = SMALL_ROWS // CHUNKS
NS, NL = len(SMALL), len(LARGE)

GROUPS = [(0, 1, 3), (4, 1, 3), (9, 1, 4), (13, 2, 2), (16, 2, 3), (21, 1, 4), (26, 1, 1)]
NG = len(GROUPS)

COLS = FEATS - 1
QUADS = BLOCK // 4
QB = 4
GRAMS = QUADS // (2 * QB)
UNF = [list(range(f, min(f + 4, COLS))) for f in range(0, COLS, 4)]
K1 = [(k, min(P, PAIR_ROWS - k)) for k in range(0, PAIR_ROWS, P)]
M1, M2 = HID1 // P, HID2 // P


def pair_offset(f):
    return f * (FEATS - 1) - f * (f - 1) // 2


def dlrm_kernel(nc, dense, ids, ids_small, tables, w1, b1, w2, b2, w3, identity, row_numbers, out):
    fp32, f32r, i32 = mybir.dt.float32, mybir.dt.float32r, mybir.dt.int32
    ALU = mybir.AluOpType
    ACT = mybir.ActivationFunctionType

    dense_v = dense.rearrange("(r t p) d -> r t p d", t=TILES, p=TILE)
    ids_v = ids.rearrange("(r t p) f -> r t p f", t=TILES, p=TILE)
    ids_small_v = ids_small.rearrange("f (r h b) -> r h f b", h=2, b=BLOCK)

    ctx = ExitStack()
    with ctx:
        def sb(name, shape, dt=fp32):
            return ctx.enter_context(nc.sbuf_tensor(name, shape, dt))

        def pb(name, shape):
            return ctx.enter_context(nc.psum_tensor(name, shape, fp32))

        def sem(name):
            return ctx.enter_context(nc.semaphore(name))

        ident = sb("ident", [P, P])
        rownum = sb("rownum", [P, CHUNKS])
        idx = sb("idx", [P, TILES, FEATS - 1], i32)
        rows = sb("rows", [P, TILES, 1 + NL, DIM])
        X = sb("X", [P, BLOCK, SLOTS])
        dense_T = sb("dense_T", [P, 2, 4, QUADS])
        table_hi = sb("table_hi", [P, NS, CHUNKS, DIM], f32r)
        table_lo = sb("table_lo", [P, NS, CHUNKS, DIM], f32r)
        ids_b = sb("ids_b", [P, 2, NS, BLOCK], i32)
        onehot = sb("onehot", [P, 2, CHUNKS, BLOCK], f32r)
        grams = sb("grams", [P, QUADS, COLS])
        pairs = sb("pairs", [QUADS, 4, PAIR_ROWS])
        pairs_T = sb("pairs_T", [P, len(K1), 4, QUADS])
        h1 = sb("h1", [P, M1, BLOCK])
        h2 = sb("h2", [P, M2, BLOCK])
        y = sb("y", [1, TURNS, 2, QUADS, 4])
        w1d = sb("w1d", [P, 2, HID1])
        w1s = sb("w1s", [P, HID1])
        w1p = sb("w1p", [P, len(K1), HID1])
        w2_sb = sb("w2_sb", [P, M1, HID2])
        w3_sb = sb("w3_sb", [P, M2])
        b1_sb = sb("b1_sb", [P, M1])
        b2_sb = sb("b2_sb", [P, M2])
        raw = X[:, :, :].rearrange("p b s -> p (b s)")[:, 0:NS * CHUNKS * DIM].rearrange(
            "p (n c d) -> p n c d", n=NS, c=CHUNKS)

        pT = pb("pT", [P, 2, 512])
        pS = pb("pS", [P, 2, 512])
        pG = pb("pG", [P, 4, 512])

        s_idx = [sem(f"s_idx{t}") for t in range(TILES)]
        s_rows = [sem(f"s_rows{t}") for t in range(TILES)]
        s_dense = [sem(f"s_dense{t}") for t in range(TILES)]
        s_ids_b = [sem(f"s_ids_b{h}") for h in range(2)]
        s_raw = [sem(f"s_raw{n}") for n in range(NS)]
        s_const = sem("s_const")
        s_w = sem("s_w")
        s_out = sem("s_out")
        s_pool_gate = sem("s_pool_gate")
        s_pe_gate = sem("s_pe_gate")
        s_hi = sem("s_hi")
        s_lo = sem("s_lo")
        s_prep = sem("s_prep")
        s_tr = sem("s_tr")
        s_tr_dve = sem("s_tr_dve")
        s_tr_act = sem("s_tr_act")
        s_onehot = sem("s_onehot")
        s_sel = sem("s_sel")
        s_sel_out = sem("s_sel_out")
        s_gram = sem("s_gram")
        s_gram_dve = sem("s_gram_dve")
        s_gram_act = sem("s_gram_act")
        s_unf = sem("s_unf")
        s_unf_out = sem("s_unf_out")
        s_pt = sem("s_pt")
        s_pt_out = sem("s_pt_out")
        s_m1 = sem("s_m1")
        s_h1 = sem("s_h1")
        s_m2 = sem("s_m2")
        s_h2 = sem("s_h2")
        s_m3 = sem("s_m3")
        s_y = sem("s_y")

        NU, NK = len(UNF), len(K1)

        def nth(r, h, per_block, i):
            return r * (2 * per_block) + (h * per_block + i + 1)

        def tile_read(r, t):
            return (r - 1) * (TILES * NG) + (t + 1) * NG

        def turns(engine, turn):
            turn(0, True, False)
            with engine.Fori(1, TURNS - 1) as r:
                turn(r, False, False)
            turn(TURNS - 1, False, True)

        block = ctx.enter_context(nc.Block())

        @block.sync
        def _(sp):
            def load_idx(r, t):
                sp.dma_start(idx[:, t, :], ids_v[r, t]).then_inc(s_idx[t], 16)

            def load_dense(r, t):
                sp.dma_start(rows[:, t, 0, :], dense_v[r, t]).then_inc(s_dense[t], 16)

            def load_ids_b(r, h):
                sp.dma_start(ids_b[:, h], ids_small_v[r, h][None].broadcast_to([P, NS, BLOCK])).then_inc(
                    s_ids_b[h], 16)

            load_idx(0, 0)
            sp.dma_start(rownum[:, :], row_numbers).then_inc(s_const, 16)
            sp.dma_start(ident[:, :], identity).then_inc(s_const, 16)
            for t in range(1, TILES):
                load_idx(0, t)
            load_ids_b(0, 0)
            for n in range(NS):
                sp.dma_start(raw[0:ROWS_P, n], tables[SMALL[n]].rearrange("(p c) d -> p c d", c=CHUNKS)).then_inc(
                    s_raw[n], 16)
            for t in range(TILES):
                load_dense(0, t)
            load_ids_b(0, 1)
            sp.dma_start(w1d[:, 0, :], w1[0:P, :]).then_inc(s_w, 16)
            sp.dma_start(w1d[:, 1, :], w1[P + PAIR_ROWS:, :]).then_inc(s_w, 16)
            for i, (k, n) in enumerate(K1):
                sp.dma_start(w1p[0:n, i, :], w1[P + k:P + k + n, :]).then_inc(s_w, 16)
            sp.dma_start(w2_sb[:, :, :], w2.rearrange("(m p) n -> p m n", p=P)).then_inc(s_w, 16)
            sp.dma_start(w3_sb[:, :], w3).then_inc(s_w, 16)
            sp.dma_start(b1_sb[:, :], b1).then_inc(s_w, 16)
            sp.dma_start(b2_sb[:, :], b2).then_inc(s_w, 16)

            with sp.Fori(1, TURNS) as r:
                for h in range(2):
                    for t in (2 * h, 2 * h + 1):
                        sp.wait_ge(s_rows[t], r * (16 * NL))
                        load_idx(r, t)
                    sp.wait_ge(s_onehot, (r - 1) * (2 * NS) + (h + 1) * NS)
                    load_ids_b(r, h)
                    for t in (2 * h, 2 * h + 1):
                        sp.wait_ge(s_tr, tile_read(r, t))
                        load_dense(r, t)
            sp.wait_ge(s_y, 2 * TURNS)
            sp.dma_start(out.rearrange("b o -> o b"),
                         y[:, :, :, :, :].rearrange("p r h q s -> p (r h q s)")).then_inc(s_out, 16)
            sp.wait_ge(s_out, 16)

        @block.gpsimd
        def _(pool):
            def gather_turn(r, first, last):
                for t in range(TILES):
                    pool.wait_ge(s_idx[t], r * 16 + 16)
                    if not first:
                        pool.wait_ge(s_tr, tile_read(r, t))
                    pool.sem_inc(s_pool_gate, 1)
                    for i, f in enumerate(LARGE):
                        nc.gpsimd.indirect_dma_start(
                            out=rows[:, t, 1 + i, :], out_offset=None, in_=tables[f],
                            in_offset=bass.IndirectOffsetOnAxis(ap=idx[:, t, f:f + 1], axis=0),
                        ).then_inc(s_rows[t], 16)

            turns(pool, gather_turn)

        def tile_of_X(t):
            return X[:, (t % 2) * TILE:(t % 2 + 1) * TILE, :]

        def group_out(copy, t, i, bank):
            f0, step, n = GROUPS[i]
            src = pT[:, bank, 0:n * TILE].rearrange("p (f b) -> p f b", f=n)
            dst = tile_of_X(t)[:, :, f0:f0 + step * (n - 1) + 1:step].rearrange("p b f -> p f b")
            last = copy(dst, src)
            if i == 0:
                q0 = (t % 2) * (QUADS // 2)
                last = copy(dense_T[:, t // 2, :, q0:q0 + QUADS // 2],
                            pT[:, bank, 0:TILE].rearrange("p (q s) -> p s q", s=4))
            return last

        def groups_of(h, parity):
            for n in range(2 * NG):
                if n % 2 == parity:
                    yield 2 * h + n // NG, n % NG, n

        def gram_out(copy, k, bank):
            for s in range(4):
                q = slice(32 * s, 32 * s + 32)
                src = pG[q, 2 * bank:2 * bank + 2, 0:QB * 4 * COLS].rearrange(
                    "p b (q s f) -> p b q s f", q=QB, s=4)[:, :, :, s, :]
                dst = grams[q, 2 * QB * k:2 * QB * (k + 1), :].rearrange("p (b q) f -> p b q f", b=2)
                last = copy(dst, src)
            return last

        @block.scalar
        def _(act):
            def copy(dst, src):
                return nc.scalar.copy(dst, src)

            for n in range(NS):
                act.wait_ge(s_raw[n], 16)
                nc.scalar.copy(table_hi[0:ROWS_P, n], raw[0:ROWS_P, n]).then_inc(s_hi, 1)

            def select_out(r, h, n):
                act.wait_ge(s_sel, nth(r, h, NS, n))
                nc.scalar.copy(X[:, :, 1 + SMALL[n]], pS[:, (h * NS + n) % 2, 0:BLOCK]).then_inc(s_sel_out, 1)

            def pairs_T_out(r, h):
                for k, (_, n) in enumerate(K1):
                    act.wait_ge(s_pt, nth(r, h, NK, k))
                    nc.scalar.copy(pairs_T[0:n, k],
                                   pG[0:n, (NU + k) % 4, 0:BLOCK].rearrange("p (s q) -> p s q", s=4)).then_inc(
                        s_pt_out, 1)

            def h1_out(r, h):
                for m in range(M1):
                    act.wait_ge(s_m1, nth(r, h, M1, m))
                    nc.scalar.activation(h1[:, m, :], pG[:, (NU + NK + m) % 4, 0:BLOCK], ACT.Relu,
                                         bias=b1_sb[:, m:m + 1]).then_inc(s_h1, 1)

            def h2_out(r, h):
                for m in range(M2):
                    act.wait_ge(s_m2, nth(r, h, M2, m))
                    nc.scalar.activation(h2[:, m, :], pG[:, (NU + NK + M1 + m) % 4, 0:BLOCK], ACT.Relu,
                                         bias=b2_sb[:, m:m + 1]).then_inc(s_h2, 1)

            def y_out(r, h):
                act.wait_ge(s_m3, nth(r, h, 1, 0))
                nc.scalar.copy(y[:, r, h], pG[0:1, (NU + NK + M1 + M2) % 4, 0:BLOCK].rearrange(
                    "p (s q) -> p q s", s=4)).then_inc(s_y, 1)

            def finish(r, h, between):
                pairs_T_out(r, h)
                between(2)
                h1_out(r, h)
                between(4)
                h2_out(r, h)
                between(6)
                y_out(r, h)

            def turn(r, first, last):
                for h in range(2):
                    def selects(n0):
                        for n in range(n0, min(n0 + 2, NS)):
                            select_out(r, h, n)
                    if first and h == 0:
                        act.wait_ge(s_prep, 1)
                    selects(0)
                    if first and h == 0:
                        for n0 in (2, 4, 6):
                            selects(n0)
                        act.wait_ge(s_w, 16 * (6 + NK))
                    else:
                        finish(r if h else r - 1, 1 - h, selects)
                    for t, i, n in groups_of(h, 1):
                        act.wait_ge(s_tr, nth(r, h, 2 * NG, n))
                        group_out(copy, t, i, 1).then_inc(s_tr_act, 1)
                    for k in range(1, GRAMS, 2):
                        act.wait_ge(s_gram, nth(r, h, GRAMS, k))
                        gram_out(copy, k, 1).then_inc(s_gram_act, 1)

            turns(act, turn)
            finish(TURNS - 1, 1, lambda n0: None)

        @block.vector
        def _(dve):
            def copy(dst, src):
                return nc.vector.tensor_copy(dst, src)

            for n in range(NS):
                dve.wait_ge(s_hi, n + 1)
                nc.vector.tensor_tensor(table_lo[0:ROWS_P, n], raw[0:ROWS_P, n],
                                        table_hi[0:ROWS_P, n].bitcast(fp32), ALU.subtract).then_inc(s_lo, 1)
            dve.wait_ge(s_lo, NS)
            nc.vector.memset(X[:, :, FEATS:SLOTS], 0.0).then_inc(s_prep, 1)
            dve.wait_ge(s_w, 16 * (6 + NK))
            nc.vector.tensor_tensor(w1s[:, :], w1d[:, 0, :], w1d[:, 1, :], ALU.add).then_inc(s_prep, 1)
            dve.wait_ge(s_const, 32)

            def make_onehot(r, h, n):
                if n == 0:
                    dve.wait_ge(s_ids_b[h], r * 16 + 16)
                i = h * NS + n
                if not (isinstance(r, int) and r == 0 and i < 2):
                    dve.wait_ge(s_sel, r * (2 * NS) + (i - 1))
                for c in range(CHUNKS):
                    last = nc.vector.tensor_scalar(onehot[0:ROWS_P, i % 2, c, :], ids_b[0:ROWS_P, h, n, :],
                                                   rownum[0:ROWS_P, c:c + 1], None, ALU.is_equal)
                last.then_inc(s_onehot, 1)

            def unfold_out(r, h):
                for u, fs in enumerate(UNF):
                    dve.wait_ge(s_unf, nth(r, h, NU, u))
                    for j, f in enumerate(fs):
                        src = pG[0:QUADS, u % 4, j * P:(j + 1) * P].rearrange("q (s g) -> q s g", s=4)
                        n = FEATS - 1 - f
                        last = nc.vector.tensor_copy(pairs[:, :, pair_offset(f):pair_offset(f) + n],
                                                     src[:, :, f + 1:FEATS])
                    last.then_inc(s_unf_out, 1)

            def turn(r, first, last):
                for h in range(2):
                    if first and h == 0:
                        make_onehot(0, 0, 0)
                        make_onehot(0, 0, 1)
                    else:
                        unfold_out(r if h else r - 1, 1 - h)
                    for n in range(2, NS):
                        make_onehot(r, h, n)
                    for t, i, n in groups_of(h, 0):
                        dve.wait_ge(s_tr, nth(r, h, 2 * NG, n))
                        group_out(copy, t, i, 0).then_inc(s_tr_dve, 1)
                    for k in range(0, GRAMS, 2):
                        dve.wait_ge(s_gram, nth(r, h, GRAMS, k))
                        gram_out(copy, k, 0).then_inc(s_gram_dve, 1)
                    if not (last and h == 1):
                        for n in range(2):
                            make_onehot(r + h, 1 - h, n)

            turns(dve, turn)
            unfold_out(TURNS - 1, 1)

        @block.tensor
        def _(pe):
            def select(r, h, n):
                i = h * NS + n
                pe.wait_ge(s_onehot, nth(r, h, NS, n))
                if not (isinstance(r, int) and r == 0 and i < 2):
                    pe.wait_ge(s_sel_out, r * (2 * NS) + (i - 1))
                for part in (table_hi, table_lo):
                    for c in range(CHUNKS):
                        last = nc.tensor.matmul(pS[:, i % 2, 0:BLOCK], part[0:ROWS_P, n, c, :],
                                                onehot[0:ROWS_P, i % 2, c, :],
                                                start=part is table_hi and c == 0,
                                                stop=part is table_lo and c == CHUNKS - 1)
                last.then_inc(s_sel, 1)

            def transposes(r, h, t):
                pe.wait_ge(s_dense[t], r * 16 + 16)
                pe.wait_ge(s_rows[t], r * (16 * NL) + 16 * NL)
                slot = {0: 0}
                for j, f in enumerate(LARGE):
                    slot[1 + f] = 1 + j
                for i, (f0, step, cnt) in enumerate(GROUPS):
                    n = (t % 2) * NG + i
                    if not (isinstance(r, int) and r == 0 and h == 0 and n < 2):
                        pe.wait_ge(s_tr_act if n % 2 else s_tr_dve,
                                   r * (2 * NG) + (h * NG + n // 2))
                    for j in range(cnt):
                        last = nc.tensor.transpose(pT[:, n % 2, j * TILE:(j + 1) * TILE],
                                                   rows[:, t, slot[f0 + j * step], :], ident[:, :])
                    last.then_inc(s_tr, 1)

            def gram(r, h):
                pe.wait_ge(s_sel_out, nth(r, h, NS, NS - 1))
                pe.wait_ge(s_tr_dve, nth(r, h, NG, NG - 1))
                pe.wait_ge(s_tr_act, nth(r, h, NG, NG - 1))
                if not (isinstance(r, int) and r == 0 and h == 0):
                    pe.wait_ge(s_y, r * 2 + h)
                for k in range(GRAMS):
                    if not (isinstance(r, int) and r == 0 and h == 0 and k < 2):
                        pe.wait_ge(s_gram_act if k % 2 else s_gram_dve,
                                   r * GRAMS + (h * (GRAMS // 2) + k // 2))
                    for b in range(2):
                        for j in range(QB):
                            s0 = 4 * (2 * QB * k + QB * b + j)
                            last = nc.tensor.matmul(
                                pG[:, 2 * (k % 2) + b, j * 4 * COLS:(j + 1) * 4 * COLS],
                                X[:, s0:s0 + 4, :].rearrange("p b s -> p (b s)"),
                                X[:, s0:s0 + 4, 0:COLS], start=True, stop=True)
                    last.then_inc(s_gram, 1)

            def unfold(r, h):
                pe.wait_ge(s_gram_dve, r * GRAMS + (h + 1) * (GRAMS // 2))
                pe.wait_ge(s_gram_act, r * GRAMS + (h + 1) * (GRAMS // 2))
                pe.sem_inc(s_pe_gate, 1)
                for u, fs in enumerate(UNF):
                    if u >= 4:
                        pe.wait_ge(s_unf_out, nth(r, h, NU, u - 4))
                        pe.sem_inc(s_pe_gate, 1)
                    for j, f in enumerate(fs):
                        last = nc.tensor.transpose(pG[0:QUADS, u % 4, j * P:(j + 1) * P],
                                                   grams[:, :, f], ident[:, :])
                    last.then_inc(s_unf, 1)

            def pair_transposes(r, h):
                pe.wait_ge(s_unf_out, nth(r, h, NU, NU - 1))
                pe.sem_inc(s_pe_gate, 1)
                for k, (k0, n) in enumerate(K1):
                    for s in range(4):
                        last = nc.tensor.transpose(pG[0:n, (NU + k) % 4, s * QUADS:(s + 1) * QUADS],
                                                   pairs[:, s, k0:k0 + n], ident[0:QUADS, 0:QUADS])
                    last.then_inc(s_pt, 1)

            def layer1(r, h):
                pe.wait_ge(s_pt_out, nth(r, h, NK, NK - 1))
                for m in range(M1):
                    dst = pG[:, (NU + NK + m) % 4, 0:BLOCK]
                    cols = slice(m * P, (m + 1) * P)
                    nc.tensor.matmul(dst, w1s[:, cols], dense_T[:, h].rearrange("p s q -> p (s q)"),
                                     start=True, stop=False)
                    for k, (_, n) in enumerate(K1):
                        last = nc.tensor.matmul(dst, w1p[0:n, k, cols],
                                                pairs_T[0:n, k].rearrange("p s q -> p (s q)"),
                                                start=False, stop=k == NK - 1)
                    last.then_inc(s_m1, 1)

            def layer2(r, h):
                pe.wait_ge(s_h1, nth(r, h, M1, M1 - 1))
                for m in range(M2):
                    for k in range(M1):
                        last = nc.tensor.matmul(pG[:, (NU + NK + M1 + m) % 4, 0:BLOCK],
                                                w2_sb[:, k, m * P:(m + 1) * P], h1[:, k, :],
                                                start=k == 0, stop=k == M1 - 1)
                    last.then_inc(s_m2, 1)

            def layer3(r, h):
                pe.wait_ge(s_h2, nth(r, h, M2, M2 - 1))
                for k in range(M2):
                    last = nc.tensor.matmul(pG[0:1, (NU + NK + M1 + M2) % 4, 0:BLOCK], w3_sb[:, k:k + 1],
                                            h2[:, k, :], start=k == 0, stop=k == M2 - 1)
                last.then_inc(s_m3, 1)

            def finish(r, h, between):
                unfold(r, h)
                between(0)
                pair_transposes(r, h)
                between(2)
                layer1(r, h)
                between(4)
                layer2(r, h)
                between(6)
                layer3(r, h)

            def turn(r, first, last):
                for h in range(2):
                    def selects(n0):
                        for n in range(n0, min(n0 + 2, NS)):
                            select(r, h, n)
                    if first and h == 0:
                        pe.wait_ge(s_lo, NS)
                        pe.wait_ge(s_const, 32)
                        for n0 in (0, 2, 4, 6):
                            selects(n0)
                        pe.wait_ge(s_w, 16 * (6 + NK))
                        pe.wait_ge(s_prep, 2)
                    else:
                        finish(r if h else r - 1, 1 - h, selects)
                    for t in (2 * h, 2 * h + 1):
                        transposes(r, h, t)
                    gram(r, h)

            turns(pe, turn)
            finish(TURNS - 1, 1, lambda n0: None)


_TABLES = [f"tbl_{i}" for i in range(FEATS - 1)]


def kernel(**inputs):
    import numpy as _np
    import concourse.bacc as _bacc
    from concourse import mybir as _mybir
    from concourse.bass_utils import run_bass_kernel_spmd as _run

    nc = _bacc.Bacc("TRN2", target_bir_lowering=False, num_devices=1)
    arrays = {}

    def dram(name, a):
        a = _np.ascontiguousarray(a)
        arrays[f"in_{name}"] = a
        return nc.dram_tensor(f"in_{name}", a.shape, _mybir.dt.from_np(a.dtype), kind="ExternalInput").ap()

    def columns(name, a):
        return dram(name, _np.asarray(a).reshape(-1, P).T)

    ids = _np.asarray(inputs["ids"])
    out = nc.dram_tensor("out", (BATCH, 1), _mybir.dt.float32, kind="ExternalOutput").ap()
    dlrm_kernel(
        nc, dram("dense", inputs["r_dense_features"]), dram("ids", ids),
        dram("ids_small", ids[:, SMALL].T), [dram(n, inputs[n]) for n in _TABLES],
        dram("w1", inputs["W_top1"]), columns("b1", inputs["b_top1"]), dram("w2", inputs["W_top2"]),
        columns("b2", inputs["b_top2"]), columns("w3", inputs["W_top3"]),
        dram("identity", _np.eye(P, dtype=_np.float32)),
        dram("row_numbers", _np.arange(P * CHUNKS, dtype=_np.float32).reshape(P, CHUNKS)), out)
    r = _run(nc, [arrays], core_ids=[0])
    return r.results[0]["out"]
```

```python
import concourse.bass as bass
from concourse import mybir
from contextlib import ExitStack

P = 128
BATCH = 2048
DIM = 128
FEATS = 27
TILE = 128
TILES = 4
BLOCK = 2 * TILE
PAIR_ROWS = FEATS * (FEATS - 1) // 2
TURNS = BATCH // (TILES * TILE)
HID1, HID2 = 512, 256

SMALL = [2, 6, 7, 13, 16, 18, 24]
LARGE = [f for f in range(FEATS - 1) if f not in SMALL]
SMALL_ROWS = 1000
CHUNKS = 8
ROWS_P = SMALL_ROWS // CHUNKS
NS, NL = len(SMALL), len(LARGE)

GROUPS = [(0, 1, 3), (4, 1, 3), (9, 1, 4), (13, 2, 2), (16, 2, 3), (21, 1, 4), (26, 1, 1)]
NG = len(GROUPS)

COLS = FEATS - 1
QUADS = BLOCK // 4
QF = 4 * FEATS
QB = 4
GRAMS = QUADS // (2 * QB)
GRAMS_DVE = [1, 5]
GRAMS_ACT = [k for k in range(GRAMS) if k not in GRAMS_DVE]
UNF = [list(range(f, min(f + 8, COLS))) for f in range(0, COLS, 8)]
UNF_DVE, UNF_ACT = [2], [0, 1, 3]
K1 = [(k, min(P, PAIR_ROWS - k)) for k in range(0, PAIR_ROWS, P)]
M1, M2 = HID1 // P, HID2 // P

TR_BANKS = [0, 1, 2, 3]
SEL_BANKS = [2, 3]
GRAM_BANKS = [4, 6, 0]
UNF_BANKS = [4, 5, 6, 7]
PT_BANKS = [4, 5, 6]
M1_BANKS = [7, 4, 5, 6]
M2_BANKS = [7, 4]
M3_BANK = 5


def pair_offset(f):
    return f * (FEATS - 1) - f * (f - 1) // 2


def dlrm_kernel(nc, dense, ids, ids_small, tables, w1, b1, w2, b2, w3, identity, minus_first_row, out):
    fp32, f32r, i32 = mybir.dt.float32, mybir.dt.float32r, mybir.dt.int32
    ALU = mybir.AluOpType
    ACT = mybir.ActivationFunctionType

    dense_v = dense.rearrange("(r t p) d -> r t p d", t=TILES, p=TILE)
    ids_v = ids.rearrange("(r t p) f -> r t p f", t=TILES, p=TILE)
    ids_small_v = ids_small.rearrange("f (r h b) -> r h f b", h=2, b=BLOCK)

    ctx = ExitStack()
    with ctx:
        def sb(name, shape, dt=fp32):
            return ctx.enter_context(nc.sbuf_tensor(name, shape, dt))

        def pb(name, shape):
            return ctx.enter_context(nc.psum_tensor(name, shape, fp32))

        def sem(name):
            return ctx.enter_context(nc.semaphore(name))

        ident = sb("ident", [P, P])
        first_row = sb("first_row", [P, 1])
        idx = sb("idx", [P, TILES, FEATS - 1], i32)
        rows = sb("rows", [P, TILES, 1 + NL, DIM])
        X = sb("X", [P, BLOCK, FEATS])
        dense_T = sb("dense_T", [P, 2, 4, QUADS])
        table_hi = sb("table_hi", [P, NS, CHUNKS, DIM], f32r)
        table_lo = sb("table_lo", [P, NS, CHUNKS, DIM], f32r)
        ids_i = sb("ids_i", [P, NS, BLOCK], i32)
        ids_f = sb("ids_f", [P, NS, BLOCK])
        onehot = sb("onehot", [P, 2, CHUNKS, BLOCK], f32r)
        grams = sb("grams", [P, COLS, QUADS])
        pairs = sb("pairs", [QUADS, 4, PAIR_ROWS])
        pairs_T = sb("pairs_T", [P, len(K1), 4, QUADS])
        h1 = sb("h1", [P, M1, BLOCK])
        h2 = sb("h2", [P, M2, BLOCK])
        y = sb("y", [1, TURNS, 2, QUADS, 4])
        w1d = sb("w1d", [P, 2, HID1])
        w1s = sb("w1s", [P, HID1])
        w1p = sb("w1p", [P, len(K1), HID1])
        w2_sb = sb("w2_sb", [P, M1, HID2])
        w3_sb = sb("w3_sb", [P, M2])
        b1_sb = sb("b1_sb", [P, M1])
        b2_sb = sb("b2_sb", [P, M2])
        ROOM = TILES // 2 * (1 + NL) // CHUNKS
        rows_23 = rows[:, 2:4].rearrange("p t f d -> p (t f d)")
        raw = [rows_23[:, n * CHUNKS * DIM:(n + 1) * CHUNKS * DIM] for n in range(ROOM)]
        raw += [grams[:, :, :].rearrange("p f q -> p (f q)")[:, 0:CHUNKS * DIM],
                h1[:, :, :].rearrange("p m b -> p (m b)")]
        raw = [x.rearrange("p (c d) -> p c d", c=CHUNKS) for x in raw]

        ps = pb("ps", [P, 8, 512])

        s_idx = [sem(f"s_idx{t}") for t in range(TILES)]
        s_rows = [sem(f"s_rows{t}") for t in range(TILES)]
        s_dense = [sem(f"s_dense{t}") for t in range(TILES)]
        s_ids_i = sem("s_ids_i")
        s_raw = [sem(f"s_raw{n}") for n in range(NS)]
        s_const = sem("s_const")
        s_w = sem("s_w")
        s_out = sem("s_out")
        s_pool_gate = sem("s_pool_gate")
        s_pe_gate = sem("s_pe_gate")
        s_hi = sem("s_hi")
        s_lo = sem("s_lo")
        s_prep = sem("s_prep")
        s_tr = sem("s_tr")
        s_tr_dve = sem("s_tr_dve")
        s_tr_act = sem("s_tr_act")
        s_ids_f = sem("s_ids_f")
        s_onehot = sem("s_onehot")
        s_sel = sem("s_sel")
        s_sel_out = sem("s_sel_out")
        s_gram = sem("s_gram")
        s_block_dve = sem("s_block_dve")
        s_block_act = sem("s_block_act")
        s_gram_dve = sem("s_gram_dve")
        s_gram_act = sem("s_gram_act")
        s_unf = sem("s_unf")
        s_unf_dve = sem("s_unf_dve")
        s_unf_act = sem("s_unf_act")
        s_pt = sem("s_pt")
        s_pt_out = sem("s_pt_out")
        s_m1 = sem("s_m1")
        s_h1 = sem("s_h1")
        s_m2 = sem("s_m2")
        s_h2 = sem("s_h2")
        s_m3 = sem("s_m3")
        s_y = sem("s_y")

        NU, NK = len(UNF), len(K1)

        def nth(r, h, per_block, i):
            return r * (2 * per_block) + (h * per_block + i + 1)

        def tile_read(r, t):
            return (r - 1) * (TILES * NG) + (t + 1) * NG

        def turns(engine, turn):
            turn(0, True, False)
            with engine.Fori(1, TURNS - 1) as r:
                turn(r, False, False)
            turn(TURNS - 1, False, True)

        block = ctx.enter_context(nc.Block())

        @block.sync
        def _(sp):
            def load_idx(r, t):
                sp.dma_start(idx[:, t, :], ids_v[r, t]).then_inc(s_idx[t], 16)

            def load_dense(r, t):
                sp.dma_start(rows[:, t, 0, :], dense_v[r, t]).then_inc(s_dense[t], 16)

            def load_ids_i(r, h):
                sp.dma_start(ids_i[:, :, :], ids_small_v[r, h][None].broadcast_to([P, NS, BLOCK])).then_inc(
                    s_ids_i, 16)

            load_idx(0, 0)
            sp.dma_start(first_row[:, :], minus_first_row).then_inc(s_const, 16)
            load_ids_i(0, 0)
            for n in range(NS):
                sp.dma_start(raw[n][0:ROWS_P], tables[SMALL[n]].rearrange("(p c) d -> p c d", c=CHUNKS)).then_inc(
                    s_raw[n], 16)
            load_idx(0, 1)
            sp.dma_start(ident[:, :], identity).then_inc(s_const, 16)
            load_dense(0, 0)
            load_dense(0, 1)
            for t in range(2, TILES):
                load_idx(0, t)
            sp.dma_start(w1d[:, 0, :], w1[0:P, :]).then_inc(s_w, 16)
            sp.dma_start(w1d[:, 1, :], w1[P + PAIR_ROWS:, :]).then_inc(s_w, 16)
            for i, (k, n) in enumerate(K1):
                sp.dma_start(w1p[0:n, i, :], w1[P + k:P + k + n, :]).then_inc(s_w, 16)
            sp.dma_start(w2_sb[:, :, :], w2.rearrange("(m p) n -> p m n", p=P)).then_inc(s_w, 16)
            sp.dma_start(w3_sb[:, :], w3).then_inc(s_w, 16)
            sp.dma_start(b1_sb[:, :], b1).then_inc(s_w, 16)
            sp.dma_start(b2_sb[:, :], b2).then_inc(s_w, 16)
            sp.wait_ge(s_ids_f, 1)
            load_ids_i(0, 1)
            sp.wait_ge(s_lo, ROOM)
            load_dense(0, 2)
            load_dense(0, 3)

            with sp.Fori(1, TURNS) as r:
                for h in range(2):
                    for t in (2 * h, 2 * h + 1):
                        sp.wait_ge(s_rows[t], r * (16 * NL))
                        load_idx(r, t)
                    for t in (2 * h, 2 * h + 1):
                        sp.wait_ge(s_tr, tile_read(r, t))
                        load_dense(r, t)
                    sp.wait_ge(s_ids_f, r * 2 + h)
                    load_ids_i(r, h)
            sp.wait_ge(s_y, 2 * TURNS)
            sp.dma_start(out.rearrange("b o -> o b"),
                         y[:, :, :, :, :].rearrange("p r h q s -> p (r h q s)")).then_inc(s_out, 16)
            sp.wait_ge(s_out, 16)

        @block.gpsimd
        def _(pool):
            def gather_turn(r, first, last):
                for t in range(TILES):
                    pool.wait_ge(s_idx[t], r * 16 + 16)
                    if not first:
                        pool.wait_ge(s_tr, tile_read(r, t))
                    if first and t == 2:
                        pool.wait_ge(s_lo, ROOM)
                    pool.sem_inc(s_pool_gate, 1)
                    for i, f in enumerate(LARGE):
                        nc.gpsimd.indirect_dma_start(
                            out=rows[:, t, 1 + i, :], out_offset=None, in_=tables[f],
                            in_offset=bass.IndirectOffsetOnAxis(ap=idx[:, t, f:f + 1], axis=0),
                        ).then_inc(s_rows[t], 16)

            turns(pool, gather_turn)

        def tile_of_X(t):
            return X[:, (t % 2) * TILE:(t % 2 + 1) * TILE, :]

        def group_out(copy, t, i, n):
            f0, step, cnt = GROUPS[i]
            bank = TR_BANKS[n % 4]
            src = ps[:, bank, 0:cnt * TILE].rearrange("p (f b) -> p f b", f=cnt)
            dst = tile_of_X(t)[:, :, f0:f0 + step * (cnt - 1) + 1:step].rearrange("p b f -> p f b")
            last = copy(dst, src)
            if i == 0:
                q0 = (t % 2) * (QUADS // 2)
                last = copy(dense_T[:, t // 2, :, q0:q0 + QUADS // 2],
                            ps[:, bank, 0:TILE].rearrange("p (q s) -> p s q", s=4))
            return last

        def groups_of(h, half, parity):
            for n in range(half * NG, (half + 1) * NG):
                if n % 2 == parity:
                    yield 2 * h + half, n % NG, n

        def gram_out(engine, copy, landed, r, h, mine, k):
            bank = GRAM_BANKS[k % 3]
            for s in reversed(range(4)):
                q = slice(0, FEATS * (s + 1))
                src = ps[q, bank:bank + 2, 0:QB * 4 * COLS].rearrange(
                    "p b (q s f) -> p b q s f", q=QB, s=4)[:, :, :, s, :]
                dst = grams[q, :, 2 * QB * k:2 * QB * (k + 1)].rearrange("p f (b q) -> p b q f", b=2)
                last = copy(dst, src)
                if s:
                    last.then_inc(landed, 1)
                    engine.wait_ge(landed, nth(r, h, 3 * len(mine), 3 * mine.index(k) + 3 - s))
            return last

        def unfold_group_out(copy, u):
            for j, f in enumerate(UNF[u]):
                half = slice((j % 2) * QUADS, (j % 2 + 1) * QUADS)
                src = ps[half, UNF_BANKS[u], j // 2 * QF:(j // 2 + 1) * QF].rearrange("q (s g) -> q s g", s=4)
                last = copy(pairs[:, :, pair_offset(f):pair_offset(f) + FEATS - 1 - f], src[:, :, f + 1:FEATS])
            return last

        def in_block_order(early, transposed, multiplied):
            for step in ((transposed, 0), (multiplied, 0), (transposed, 1), (multiplied, 1)) if early else (
                    (transposed, 0), (transposed, 1), (multiplied, 0), (multiplied, 1)):
                step[0](step[1])

        def is_early(first, last, h):
            return (first and h == 0) or (last and h == 1)

        @block.scalar
        def _(act):
            def copy(dst, src):
                return nc.scalar.copy(dst, src)

            def ids_to_float(r, h):
                act.wait_ge(s_ids_i, r * 32 + (16 * h + 16))
                if not (isinstance(r, int) and r == 0 and h == 0):
                    act.wait_ge(s_onehot, r * (2 * NS) + h * NS)
                nc.scalar.activation(ids_f[:, :, :], ids_i[:, :, :], ACT.Identity, bias=first_row[:, 0:1]).then_inc(
                    s_ids_f, 1)

            act.wait_ge(s_const, 16)
            ids_to_float(0, 0)
            for n in range(NS):
                act.wait_ge(s_raw[n], 16)
                nc.scalar.copy(table_hi[0:ROWS_P, n], raw[n][0:ROWS_P]).then_inc(s_hi, 1)

            def select_out(r, h, n):
                act.wait_ge(s_sel, nth(r, h, NS, n))
                nc.scalar.copy(X[:, :, 1 + SMALL[n]], ps[:, SEL_BANKS[(h * NS + n) % 2], 0:BLOCK]).then_inc(s_sel_out, 1)

            def pairs_T_out(r, h):
                for k, (_, n) in enumerate(K1):
                    act.wait_ge(s_pt, nth(r, h, NK, k))
                    nc.scalar.copy(pairs_T[0:n, k],
                                   ps[0:n, PT_BANKS[k], 0:BLOCK].rearrange("p (s q) -> p s q", s=4)).then_inc(
                        s_pt_out, 1)

            def h1_out(r, h):
                for m in range(M1):
                    act.wait_ge(s_m1, nth(r, h, M1, m))
                    nc.scalar.activation(h1[:, m, :], ps[:, M1_BANKS[m], 0:BLOCK], ACT.Relu,
                                         bias=b1_sb[:, m:m + 1]).then_inc(s_h1, 1)

            def h2_out(r, h):
                for m in range(M2):
                    act.wait_ge(s_m2, nth(r, h, M2, m))
                    nc.scalar.activation(h2[:, m, :], ps[:, M2_BANKS[m], 0:BLOCK], ACT.Relu,
                                         bias=b2_sb[:, m:m + 1]).then_inc(s_h2, 1)

            def y_out(r, h):
                act.wait_ge(s_m3, nth(r, h, 1, 0))
                nc.scalar.copy(y[:, r, h], ps[0:1, M3_BANK, 0:BLOCK].rearrange(
                    "p (s q) -> p q s", s=4)).then_inc(s_y, 1)

            def unfold_out(r, h):
                for i, u in enumerate(UNF_ACT):
                    act.wait_ge(s_unf, nth(r, h, NU, u))
                    unfold_group_out(copy, u).then_inc(s_unf_act, 1)

            def finish(r, h, between):
                between(0, 2)
                unfold_out(r, h)
                between(2, 4)
                pairs_T_out(r, h)
                between(4, 5)
                h1_out(r, h)
                between(5, 6)
                h2_out(r, h)
                between(6, 7)
                y_out(r, h)

            def turn(r, first, last):
                for h in range(2):
                    def selects(n0, n1):
                        for n in range(n0, n1):
                            if n == NS - 1 and not (last and h == 1):
                                ids_to_float(r + h, 1 - h)
                            select_out(r, h, n)
                    if first and h == 0:
                        selects(0, NS)
                        act.wait_ge(s_w, 16 * (6 + NK))
                    else:
                        finish(r if h else r - 1, 1 - h, selects)

                    def groups(half):
                        for t, i, n in groups_of(h, half, 1):
                            act.wait_ge(s_tr, nth(r, h, 2 * NG, n))
                            group_out(copy, t, i, n).then_inc(s_tr_act, 1)

                    def gram_tile(half):
                        for k in GRAMS_ACT:
                            if k // (GRAMS // 2) == half:
                                act.wait_ge(s_gram, nth(r, h, GRAMS, k))
                                gram_out(act, copy, s_block_act, r, h, GRAMS_ACT, k).then_inc(s_gram_act, 1)

                    in_block_order(is_early(first, last, h), groups, gram_tile)

            turns(act, turn)
            finish(TURNS - 1, 1, lambda n0, n1: None)

        @block.vector
        def _(dve):
            def copy(dst, src):
                return nc.vector.tensor_copy(dst, src)

            def split_table(n):
                dve.wait_ge(s_hi, n + 1)
                nc.vector.tensor_tensor(table_lo[0:ROWS_P, n], raw[n][0:ROWS_P],
                                        table_hi[0:ROWS_P, n].bitcast(fp32), ALU.subtract).then_inc(s_lo, 1)


            def make_onehot(r, h, n):
                if n == 0:
                    dve.wait_ge(s_ids_f, r * 2 + (h + 1))
                i = h * NS + n
                if not (isinstance(r, int) and r == 0 and i < 2):
                    dve.wait_ge(s_sel, r * (2 * NS) + (i - 1))
                for c in range(CHUNKS):
                    last = nc.vector.tensor_scalar(onehot[0:ROWS_P, i % 2, c, :], ids_f[0:ROWS_P, n, :],
                                                   float(c), None, ALU.is_equal)
                last.then_inc(s_onehot, 1)

            def unfold_out(r, h):
                for u in UNF_DVE:
                    dve.wait_ge(s_unf, nth(r, h, NU, u))
                    unfold_group_out(copy, u).then_inc(s_unf_dve, 1)

            def turn(r, first, last):
                for h in range(2):
                    if first and h == 0:
                        for n in range(NS):
                            split_table(n)
                            make_onehot(0, 0, n)
                        dve.wait_ge(s_w, 16 * (6 + NK))
                        nc.vector.tensor_tensor(w1s[:, :], w1d[:, 0, :], w1d[:, 1, :], ALU.add).then_inc(s_prep, 1)
                    else:
                        make_onehot(r, h, 2)
                        unfold_out(r if h else r - 1, 1 - h)
                        for n in range(3, NS):
                            make_onehot(r, h, n)

                    def groups(half):
                        for t, i, n in groups_of(h, half, 0):
                            dve.wait_ge(s_tr, nth(r, h, 2 * NG, n))
                            group_out(copy, t, i, n).then_inc(s_tr_dve, 1)

                    def gram_tile(half):
                        if not (last and h == 1):
                            make_onehot(r + h, 1 - h, half)
                        for k in GRAMS_DVE:
                            if k // (GRAMS // 2) == half:
                                dve.wait_ge(s_gram, nth(r, h, GRAMS, k))
                                gram_out(dve, copy, s_block_dve, r, h, GRAMS_DVE, k).then_inc(s_gram_dve, 1)

                    in_block_order(is_early(first, last, h), groups, gram_tile)

            turns(dve, turn)
            unfold_out(TURNS - 1, 1)

        @block.tensor
        def _(pe):
            def select(r, h, n):
                i = h * NS + n
                pe.wait_ge(s_onehot, nth(r, h, NS, n))
                if not (isinstance(r, int) and r == 0 and i < 2):
                    pe.wait_ge(s_sel_out, r * (2 * NS) + (i - 1))
                for part in (table_hi, table_lo):
                    for c in range(CHUNKS):
                        last = nc.tensor.matmul(ps[:, SEL_BANKS[i % 2], 0:BLOCK], part[0:ROWS_P, n, c, :],
                                                onehot[0:ROWS_P, i % 2, c, :],
                                                start=part is table_hi and c == 0,
                                                stop=part is table_lo and c == CHUNKS - 1)
                last.then_inc(s_sel, 1)

            def transposes(r, h, t, early):
                pe.wait_ge(s_dense[t], r * 16 + 16)
                pe.wait_ge(s_rows[t], r * (16 * NL) + 16 * NL)
                slot = {0: 0}
                for j, f in enumerate(LARGE):
                    slot[1 + f] = 1 + j
                for i, (f0, step, cnt) in enumerate(GROUPS):
                    n = (t % 2) * NG + i
                    if early and n == NG:
                        wait_gram_out(r, h, GRAMS // 2 - 2)
                    if n == 2:
                        pe.wait_ge(s_sel_out, nth(r, h, NS, NS - 1))
                    if n >= 4:
                        pe.wait_ge(s_tr_act if n % 2 else s_tr_dve,
                                   r * (2 * NG) + (h * NG + (n - 4) // 2 + 1))
                    for j in range(cnt):
                        last = nc.tensor.transpose(ps[:, TR_BANKS[n % 4], j * TILE:(j + 1) * TILE],
                                                   rows[:, t, slot[f0 + j * step], :], ident[:, :])
                    last.then_inc(s_tr, 1)

            def wait_gram_out(r, h, k):
                if k in GRAMS_DVE:
                    pe.wait_ge(s_gram_dve, nth(r, h, len(GRAMS_DVE), GRAMS_DVE.index(k)))
                else:
                    pe.wait_ge(s_gram_act, nth(r, h, len(GRAMS_ACT), GRAMS_ACT.index(k)))

            def wait_transposed(r, h, half):
                pe.wait_ge(s_tr_dve, r * (2 * NG) + (h * NG + (NG * (half + 1) + 1) // 2))
                pe.wait_ge(s_tr_act, r * (2 * NG) + (h * NG + NG * (half + 1) // 2))

            def gram(r, h, half, early):
                if half == 0:
                    pe.wait_ge(s_sel_out, nth(r, h, NS, NS - 1))
                wait_transposed(r, h, half)
                if half == 0 and not (isinstance(r, int) and r == 0 and h == 0):
                    pe.wait_ge(s_y, r * 2 + h)
                for k in range(half * GRAMS // 2, (half + 1) * GRAMS // 2):
                    if k == 2 and not early:
                        wait_transposed(r, h, 1)
                    if k >= 3:
                        wait_gram_out(r, h, k - 3)
                    for b in range(2):
                        for j in range(QB):
                            s0 = 4 * (2 * QB * k + QB * b + j)
                            last = nc.tensor.matmul(
                                ps[0:QF, GRAM_BANKS[k % 3] + b, j * 4 * COLS:(j + 1) * 4 * COLS],
                                X[:, s0:s0 + 4, :].rearrange("p b s -> p (b s)"),
                                X[:, s0:s0 + 4, 0:COLS], start=True, stop=True)
                    last.then_inc(s_gram, 1)

            def unfold(r, h):
                wait_gram_out(r, h, GRAMS_DVE[-1])
                wait_gram_out(r, h, GRAMS_ACT[-1])
                pe.sem_inc(s_pe_gate, 1)
                for u, fs in enumerate(UNF):
                    for j in range(0, len(fs), 2):
                        last = nc.tensor.transpose(
                            ps[:, UNF_BANKS[u], j // 2 * QF:(j // 2 + 1) * QF],
                            grams[0:QF, fs[j]:fs[j] + 2, :].rearrange("p f q -> p (f q)"), ident[0:QF, 0:QF])
                    last.then_inc(s_unf, 1)

            def pair_transposes(r, h):
                pe.wait_ge(s_unf_dve, nth(r, h, len(UNF_DVE), len(UNF_DVE) - 1))
                pe.wait_ge(s_unf_act, nth(r, h, len(UNF_ACT), len(UNF_ACT) - 1))
                pe.sem_inc(s_pe_gate, 1)
                for k, (k0, n) in enumerate(K1):
                    for s in range(4):
                        last = nc.tensor.transpose(ps[0:n, PT_BANKS[k], s * QUADS:(s + 1) * QUADS],
                                                   pairs[:, s, k0:k0 + n], ident[0:QUADS, 0:QUADS])
                    last.then_inc(s_pt, 1)

            def layer1(r, h):
                pe.wait_ge(s_pt_out, nth(r, h, NK, NK - 1))
                for m in range(M1):
                    dst = ps[:, M1_BANKS[m], 0:BLOCK]
                    cols = slice(m * P, (m + 1) * P)
                    nc.tensor.matmul(dst, w1s[:, cols], dense_T[:, h].rearrange("p s q -> p (s q)"),
                                     start=True, stop=False)
                    for k, (_, n) in enumerate(K1):
                        last = nc.tensor.matmul(dst, w1p[0:n, k, cols],
                                                pairs_T[0:n, k].rearrange("p s q -> p (s q)"),
                                                start=False, stop=k == NK - 1)
                    last.then_inc(s_m1, 1)

            def layer2(r, h):
                pe.wait_ge(s_h1, nth(r, h, M1, M1 - 1))
                for m in range(M2):
                    for k in range(M1):
                        last = nc.tensor.matmul(ps[:, M2_BANKS[m], 0:BLOCK],
                                                w2_sb[:, k, m * P:(m + 1) * P], h1[:, k, :],
                                                start=k == 0, stop=k == M1 - 1)
                    last.then_inc(s_m2, 1)

            def layer3(r, h):
                pe.wait_ge(s_h2, nth(r, h, M2, M2 - 1))
                for k in range(M2):
                    last = nc.tensor.matmul(ps[0:1, M3_BANK, 0:BLOCK], w3_sb[:, k:k + 1],
                                            h2[:, k, :], start=k == 0, stop=k == M2 - 1)
                last.then_inc(s_m3, 1)

            def finish(r, h, between):
                between(0, 2)
                unfold(r, h)
                between(2, 4)
                pair_transposes(r, h)
                between(4, 5)
                layer1(r, h)
                between(5, 6)
                layer2(r, h)
                between(6, 7)
                layer3(r, h)

            def turn(r, first, last):
                for h in range(2):
                    def selects(n0, n1):
                        for n in range(n0, n1):
                            if first and h == 0:
                                pe.wait_ge(s_lo, n + 1)
                            select(r, h, n)
                    if first and h == 0:
                        selects(0, NS)
                        pe.wait_ge(s_const, 32)
                    else:
                        if first:
                            pe.wait_ge(s_w, 16 * (6 + NK))
                            pe.wait_ge(s_prep, 1)
                        finish(r if h else r - 1, 1 - h, selects)
                    in_block_order(is_early(first, last, h), lambda half: transposes(r, h, 2 * h + half,
                                                                       is_early(first, last, h)),
                                   lambda half: gram(r, h, half, is_early(first, last, h)))

            turns(pe, turn)
            finish(TURNS - 1, 1, lambda n0, n1: None)


_TABLES = [f"tbl_{i}" for i in range(FEATS - 1)]


def kernel(**inputs):
    import numpy as _np
    import concourse.bacc as _bacc
    from concourse import mybir as _mybir
    from concourse.bass_utils import run_bass_kernel_spmd as _run

    nc = _bacc.Bacc("TRN2", target_bir_lowering=False, num_devices=1)
    arrays = {}

    def dram(name, a):
        a = _np.ascontiguousarray(a)
        arrays[f"in_{name}"] = a
        return nc.dram_tensor(f"in_{name}", a.shape, _mybir.dt.from_np(a.dtype), kind="ExternalInput").ap()

    def columns(name, a):
        return dram(name, _np.asarray(a).reshape(-1, P).T)

    ids = _np.asarray(inputs["ids"])
    out = nc.dram_tensor("out", (BATCH, 1), _mybir.dt.float32, kind="ExternalOutput").ap()
    dlrm_kernel(
        nc, dram("dense", inputs["r_dense_features"]), dram("ids", ids),
        dram("ids_small", ids[:, SMALL].T), [dram(n, inputs[n]) for n in _TABLES],
        dram("w1", inputs["W_top1"]), columns("b1", inputs["b_top1"]), dram("w2", inputs["W_top2"]),
        columns("b2", inputs["b_top2"]), columns("w3", inputs["W_top3"]),
        dram("identity", _np.eye(P, dtype=_np.float32)),
        dram("minus_first_row", -CHUNKS * _np.arange(P, dtype=_np.float32).reshape(P, 1)), out)
    r = _run(nc, [arrays], core_ids=[0])
    return r.results[0]["out"]
```

```python
import concourse.bass as bass
from concourse import mybir
from contextlib import ExitStack

P = 128
BATCH = 2048
DIM = 128
FEATS = 27
TILE = 128
TILES = 4
BLOCK = 2 * TILE
PAIR_ROWS = FEATS * (FEATS - 1) // 2
TURNS = BATCH // (TILES * TILE)
HID1, HID2 = 512, 256

SMALL = [2, 6, 7, 13, 16, 18, 24]
LARGE = [f for f in range(FEATS - 1) if f not in SMALL]
SMALL_ROWS = 1000
CHUNKS = 8
ROWS_P = SMALL_ROWS // CHUNKS
NS, NL = len(SMALL), len(LARGE)

GROUPS = [(0, 1, 3), (4, 1, 3), (9, 1, 4), (13, 2, 2), (16, 2, 3), (21, 1, 4), (26, 1, 1)]
NG = len(GROUPS)
GROUPS_ACT = range(0, NG, 2)
GROUPS_DVE = range(1, NG, 2)
PART_GROUPS = [0, 5, 6]
GATHERED = [max(sum(cnt for _, _, cnt in GROUPS[:g]) - 1, 0) for g in PART_GROUPS] + [NL]
PARTS = [b - a for a, b in zip(GATHERED, GATHERED[1:])]

COLS = FEATS - 1
QUADS = BLOCK // 4
QF = 4 * FEATS
QB = 4
GRAMS = QUADS // (2 * QB)
GRAMS_AHEAD = 3
GRAMS_DVE = [0, 1, 5]
GRAMS_ACT = [0, 2, 3, 4, 6, 7]
LAST_GRAMS_DVE = [0, 1, 3, 5, 7]
LAST_GRAMS_ACT = [0, 2, 4, 6, 7]
UNF = [list(range(f, min(f + 8, COLS))) for f in range(0, COLS, 8)]
UNF_DVE, UNF_ACT = [2], [0, 1, 3]
LAST_UNF_DVE, LAST_UNF_ACT = [1, 3], [0, 2]
K1 = [(k, min(P, PAIR_ROWS - k)) for k in range(0, PAIR_ROWS, P)]
M1, M2 = HID1 // P, HID2 // P

TR_BANKS = [0, 1, 2, 3]
SEL_BANKS = [2, 3]
GRAM_BANKS = [4, 6, 4, 6, 0, 4, 6, 0]
UNF_BANKS = [4, 5, 6, 7]
PT_BANKS = [4, 5, 6]
M1_BANKS = [7, 4, 5, 6]
LAST_M1_BANKS = [2, 3, 0, 1]
M2_BANKS = [7, 4]
M3_BANK = 7


def pair_offset(f):
    return f * (FEATS - 1) - f * (f - 1) // 2


def dlrm_kernel(nc, dense, ids, ids_small, tables, w1, b1, w2, b2, w3, identity, minus_first_row, out):
    fp32, f32r, i32 = mybir.dt.float32, mybir.dt.float32r, mybir.dt.int32
    ALU = mybir.AluOpType
    ACT = mybir.ActivationFunctionType

    dense_v = dense.rearrange("(r t p) d -> r t p d", t=TILES, p=TILE)
    ids_v = ids.rearrange("(r t p) f -> r t p f", t=TILES, p=TILE)
    ids_small_v = ids_small.rearrange("f (r h b) -> r h f b", h=2, b=BLOCK)

    out_v = out.rearrange("(r h b) o -> r h o b", h=2, b=BLOCK)
    NU, NK = len(UNF), len(K1)

    ctx = ExitStack()
    with ctx:
        def sb(name, shape, dt=fp32):
            return ctx.enter_context(nc.sbuf_tensor(name, shape, dt))

        def pb(name, shape):
            return ctx.enter_context(nc.psum_tensor(name, shape, fp32))

        def sem(name):
            return ctx.enter_context(nc.semaphore(name))

        ident = sb("ident", [P, P])
        first_row = sb("first_row", [P, 1])
        idx = sb("idx", [P, TILES, FEATS - 1], i32)
        rows = sb("rows", [P, TILES, 1 + NL, DIM])
        X = sb("X", [P, BLOCK, FEATS])
        dense_T = sb("dense_T", [P, 4, QUADS])
        table_hi = sb("table_hi", [P, NS, CHUNKS, DIM], f32r)
        table_lo = sb("table_lo", [P, NS, CHUNKS, DIM], f32r)
        ids_f = sb("ids_f", [P, NS, BLOCK])
        ids_i = ids_f[:, :, :].bitcast(i32)
        onehot = sb("onehot", [P, 2, CHUNKS, BLOCK], f32r)
        grams = sb("grams", [P, COLS, QUADS])
        pairs = sb("pairs", [QUADS, 4, PAIR_ROWS])
        dense_T_hi = sb("dense_T_hi", [P, 4, QUADS], f32r)
        dense_T_lo = sb("dense_T_lo", [P, 4, QUADS], f32r)
        pairs_T_hi = sb("pairs_T_hi", [P, NK, 4, QUADS], f32r)
        pairs_T_lo = sb("pairs_T_lo", [P, NK, 4, QUADS], f32r)
        h1_hi = sb("h1_hi", [P, M1, BLOCK], f32r)
        h1_lo = sb("h1_lo", [P, M1, BLOCK], f32r)
        h2 = sb("h2", [P, M2, BLOCK])
        y = sb("y", [1, 2, QUADS, 4])
        w1s_hi = sb("w1s_hi", [P, HID1], f32r)
        w1s_lo = sb("w1s_lo", [P, HID1], f32r)
        w1p_hi = sb("w1p_hi", [P, NK, HID1], f32r)
        w1p_lo = sb("w1p_lo", [P, NK, HID1], f32r)
        w2_hi = sb("w2_hi", [P, M1, HID2], f32r)
        w2_lo = sb("w2_lo", [P, M1, HID2], f32r)
        w3_sb = sb("w3_sb", [P, M2])
        b1_sb = sb("b1_sb", [P, M1])
        b2_sb = sb("b2_sb", [P, M2])
        h1 = grams[:, :, :].rearrange("p f q -> p (f q)")[:, 0:M1 * BLOCK].rearrange("p (m b) -> p m b", m=M1)

        flat = rows[:, :, :, :].rearrange("p t f d -> p t (f d)")
        ROOM = (1 + NL) * DIM
        tile_123 = flat[:, 1:4].rearrange("p t n -> p (t n)")
        raw = [tile_123[:, n * CHUNKS * DIM:(n + 1) * CHUNKS * DIM].rearrange("p (c d) -> p c d", c=CHUNKS)
               for n in range(NS)]
        in_tiles = [-(-t * ROOM // (CHUNKS * DIM)) for t in range(TILES)]
        w1p = flat[:, 3, 0:NK * HID1].rearrange("p (k n) -> p k n", k=NK)
        w2_raw = flat[:, 3, NK * HID1:NK * HID1 + M1 * HID2].rearrange("p (m n) -> p m n", m=M1)
        w1d = grams[:, :, :].rearrange("p f q -> p (f q)")[:, 0:2 * HID1].rearrange("p (i n) -> p i n", i=2)

        ps = pb("ps", [P, 8, 512])

        s_idx = [sem(f"s_idx{t}") for t in range(TILES)]
        s_rows = [[sem(f"s_rows{t}_{part}") for part in range(len(PARTS))] for t in range(TILES)]
        s_dense = [sem(f"s_dense{t}") for t in range(TILES)]
        s_ids_i = sem("s_ids_i")
        s_raw = [sem(f"s_raw{n}") for n in range(NS)]
        s_const = sem("s_const")
        s_w1d = sem("s_w1d")
        s_w = sem("s_w")
        s_w2 = sem("s_w2")
        s_bias = sem("s_bias")
        s_out = [sem(f"s_out{h}") for h in range(2)]
        s_pool_gate = sem("s_pool_gate")
        s_pe_gate = sem("s_pe_gate")
        s_sp_gate = sem("s_sp_gate")
        s_hi = sem("s_hi")
        s_lo = sem("s_lo")
        s_w_sum = sem("s_w_sum")
        s_w_hi = sem("s_w_hi")
        s_w_lo = sem("s_w_lo")
        s_tr = sem("s_tr")
        s_tr_dve = sem("s_tr_dve")
        s_tr_act = sem("s_tr_act")
        s_ids_f = sem("s_ids_f")
        s_onehot = sem("s_onehot")
        s_sel = sem("s_sel")
        s_sel_out = sem("s_sel_out")
        s_gram = sem("s_gram")
        s_block_dve = sem("s_block_dve")
        s_block_act = sem("s_block_act")
        s_gram_dve = sem("s_gram_dve")
        s_gram_act = sem("s_gram_act")
        s_unf = sem("s_unf")
        s_unf_dve = sem("s_unf_dve")
        s_unf_act = sem("s_unf_act")
        s_pt = sem("s_pt")
        s_pt_hi = sem("s_pt_hi")
        s_pt_lo = sem("s_pt_lo")
        s_m1 = sem("s_m1")
        s_h1_hi = sem("s_h1_hi")
        s_h1 = sem("s_h1")
        s_h1_lo = sem("s_h1_lo")
        s_m2 = sem("s_m2")
        s_h2 = sem("s_h2")
        s_m3 = sem("s_m3")
        s_y = sem("s_y")

        def nth(r, h, per_block, i):
            return r * (2 * per_block) + (h * per_block + i + 1)

        def tile_read(r, t):
            return (r - 1) * (TILES * NG) + (t + 1) * NG

        def is_first(r, h):
            return isinstance(r, int) and r == 0 and h == 0

        def is_last(r, h):
            return isinstance(r, int) and r == TURNS - 1 and h == 1

        def by_block(usual, in_last, r, h):
            return in_last if is_last(r, h) else usual

        def turns(engine, turn):
            turn(0)
            with engine.Fori(1, TURNS - 1) as r:
                turn(r)
            turn(TURNS - 1)

        block = ctx.enter_context(nc.Block())

        @block.sync
        def _(sp):
            def load_idx(r, t):
                sp.dma_start(idx[:, t, :], ids_v[r, t]).then_inc(s_idx[t], 16)

            def load_dense(r, t):
                sp.dma_start(rows[:, t, 0, :], dense_v[r, t]).then_inc(s_dense[t], 16)

            def load_ids_i(r, h):
                sp.dma_start(ids_i, ids_small_v[r, h][None].broadcast_to([P, NS, BLOCK])).then_inc(
                    s_ids_i, 16)

            load_idx(0, 0)
            sp.dma_start(first_row[:, :], minus_first_row).then_inc(s_const, 16)
            load_ids_i(0, 0)
            for n in range(NS):
                sp.dma_start(raw[n][0:ROWS_P], tables[SMALL[n]].rearrange("(p c) d -> p c d", c=CHUNKS)).then_inc(
                    s_raw[n], 16)
            load_dense(0, 0)
            sp.dma_start(ident[:, :], identity).then_inc(s_const, 16)
            for t in range(1, TILES):
                load_idx(0, t)
            sp.dma_start(w3_sb[:, :], w3).then_inc(s_bias, 16)
            sp.dma_start(b1_sb[:, :], b1).then_inc(s_bias, 16)
            sp.dma_start(b2_sb[:, :], b2).then_inc(s_bias, 16)
            sp.dma_start(w1d[:, 0, :], w1[0:P, :]).then_inc(s_w1d, 16)
            sp.dma_start(w1d[:, 1, :], w1[P + PAIR_ROWS:, :]).then_inc(s_w1d, 16)
            for t in (1, 2):
                sp.wait_ge(s_lo, in_tiles[t])
                load_dense(0, t)
            sp.wait_ge(s_lo, NS)
            for i, (k, n) in enumerate(K1):
                sp.dma_start(w1p[0:n, i, :], w1[P + k:P + k + n, :]).then_inc(s_w, 16)
            sp.dma_start(w2_raw, w2.rearrange("(m p) n -> p m n", p=P)).then_inc(s_w2, 16)
            sp.wait_ge(s_onehot, NS)
            load_ids_i(0, 1)
            sp.wait_ge(s_w_lo, 2 + NK)
            load_dense(0, 3)

            with sp.Fori(1, TURNS) as r:
                for h in range(2):
                    for t in (2 * h, 2 * h + 1):
                        for part in range(len(PARTS)):
                            sp.wait_ge(s_rows[t][part], r * (16 * PARTS[part]))
                            sp.sem_inc(s_sp_gate, 1)
                        load_idx(r, t)
                    for t in (2 * h, 2 * h + 1):
                        sp.wait_ge(s_tr, tile_read(r, t))
                        load_dense(r, t)
                    sp.wait_ge(s_onehot, r * (2 * NS) + h * NS)
                    load_ids_i(r, h)

        @block.gpsimd
        def _(pool):
            def gather_turn(r):
                first = is_first(r, 0)
                for t in range(TILES):
                    pool.wait_ge(s_idx[t], r * 16 + 16)
                    if not first:
                        pool.wait_ge(s_tr, tile_read(r, t))
                    if first and t in (1, 2):
                        pool.wait_ge(s_lo, in_tiles[t])
                    if first and t == 3:
                        pool.wait_ge(s_w_lo, 2 + NK)
                    pool.sem_inc(s_pool_gate, 1)
                    for i, f in enumerate(LARGE):
                        nc.gpsimd.indirect_dma_start(
                            out=rows[:, t, 1 + i, :], out_offset=None, in_=tables[f],
                            in_offset=bass.IndirectOffsetOnAxis(ap=idx[:, t, f:f + 1], axis=0),
                        ).then_inc(s_rows[t][sum(i >= g for g in GATHERED[1:])], 16)

            turns(pool, gather_turn)

        def tile_of_X(t):
            return X[:, (t % 2) * TILE:(t % 2 + 1) * TILE, :]

        def group_out(copy, t, i):
            f0, step, cnt = GROUPS[i]
            bank = TR_BANKS[i % 4]
            src = ps[:, bank, 0:cnt * TILE].rearrange("p (f b) -> p f b", f=cnt)
            dst = tile_of_X(t)[:, :, f0:f0 + step * (cnt - 1) + 1:step].rearrange("p b f -> p f b")
            last = copy(dst, src)
            if i == 0:
                q0 = (t % 2) * (QUADS // 2)
                last = copy(dense_T[:, :, q0:q0 + QUADS // 2],
                            ps[:, bank, 0:TILE].rearrange("p (q s) -> p s q", s=4))
            return last

        def gram_out(engine, copy, landed, r, h, per_block, i, k, my_bank):
            shared = k in by_block(GRAMS_DVE, LAST_GRAMS_DVE, r, h) and k in by_block(GRAMS_ACT, LAST_GRAMS_ACT, r, h)
            banks = range(my_bank, my_bank + 1) if shared else range(2)
            for s in reversed(range(4)):
                q = slice(0, FEATS * (s + 1))
                src = ps[q, GRAM_BANKS[k] + banks[0]:GRAM_BANKS[k] + banks[-1] + 1, 0:QB * 4 * COLS].rearrange(
                    "p b (q s f) -> p b q s f", q=QB, s=4)[:, :, :, s, :]
                q0 = 2 * QB * k + QB * banks[0]
                dst = grams[q, :, q0:q0 + QB * len(banks)].rearrange("p f (b q) -> p b q f", b=len(banks))
                last = copy(dst, src)
                if s:
                    last.then_inc(landed, 1)
                    engine.wait_ge(landed, nth(r, h, 3 * per_block, 3 * i + 3 - s))
            return last

        def unfold_group_out(copy, u):
            for j, f in enumerate(UNF[u]):
                half = slice((j % 2) * QUADS, (j % 2 + 1) * QUADS)
                src = ps[half, UNF_BANKS[u], j // 2 * QF:(j // 2 + 1) * QF].rearrange("q (s g) -> q s g", s=4)
                last = copy(pairs[:, :, pair_offset(f):pair_offset(f) + FEATS - 1 - f], src[:, :, f + 1:FEATS])
            return last

        @block.scalar
        def _(act):
            def copy(dst, src):
                return nc.scalar.copy(dst, src)

            act.wait_ge(s_const, 16)
            act.wait_ge(s_ids_i, 16)
            nc.scalar.activation(ids_f[:, :, :], ids_i, ACT.Identity, bias=first_row[:, 0:1]).then_inc(s_ids_f, 1)
            for n in range(NS):
                act.wait_ge(s_raw[n], 16)
                nc.scalar.copy(table_hi[0:ROWS_P, n], raw[n][0:ROWS_P]).then_inc(s_hi, 1)

            def split_pair_weights():
                act.wait_ge(s_w, 16 * NK)
                for i, (_, n) in enumerate(K1):
                    nc.scalar.copy(w1p_hi[0:n, i], w1p[0:n, i]).then_inc(s_w_hi, 1)

            def split_layer2_weights():
                act.wait_ge(s_w2, 16)
                act.wait_ge(s_bias, 48)
                nc.scalar.copy(w2_hi[:, :, :], w2_raw).then_inc(s_w_hi, 1)

            def split_dense_weights():
                act.wait_ge(s_w_sum, 1)
                nc.scalar.copy(w1s_hi[:, :], w1d[:, 0]).then_inc(s_w_hi, 1)

            def select_out(r, h, n):
                act.wait_ge(s_sel, nth(r, h, NS, n))
                nc.scalar.copy(X[:, :, 1 + SMALL[n]], ps[:, SEL_BANKS[(h * NS + n) % 2], 0:BLOCK]).then_inc(s_sel_out, 1)

            def dense_T_out():
                nc.scalar.copy(dense_T_hi[:, :, :], dense_T[:, :, :]).then_inc(s_pt_hi, 1)

            def pairs_T_out(r, h):
                for k, (_, n) in enumerate(K1):
                    act.wait_ge(s_pt, nth(r, h, NK, k))
                    nc.scalar.copy(pairs_T_hi[0:n, k],
                                   ps[0:n, PT_BANKS[k], 0:BLOCK].rearrange("p (s q) -> p s q", s=4)).then_inc(
                        s_pt_hi, 1)

            def h1_out(r, h):
                for m in range(M1):
                    act.wait_ge(s_m1, nth(r, h, M1, m))
                    nc.scalar.activation(h1_hi[:, m, :], ps[:, M1_BANKS[m], 0:BLOCK], ACT.Relu,
                                         bias=b1_sb[:, m:m + 1]).then_inc(s_h1_hi, 1)
                    nc.scalar.activation(h1[:, m, :], ps[:, M1_BANKS[m], 0:BLOCK], ACT.Relu,
                                         bias=b1_sb[:, m:m + 1]).then_inc(s_h1, 1)

            def last_h1_out(r, h):
                for m in range(M1):
                    act.wait_ge(s_m1, nth(r, h, M1, m))
                    nc.scalar.activation(h1_hi[:, m, :], ps[:, LAST_M1_BANKS[m], 0:BLOCK], ACT.Relu,
                                         bias=b1_sb[:, m:m + 1]).then_inc(s_h1_hi, 1)

            def h2_out(r, h):
                for m in range(M2):
                    act.wait_ge(s_m2, nth(r, h, M2, m))
                    nc.scalar.activation(h2[:, m, :], ps[:, M2_BANKS[m], 0:BLOCK], ACT.Relu,
                                         bias=b2_sb[:, m:m + 1]).then_inc(s_h2, 1)

            def y_out(r, h):
                act.wait_ge(s_m3, nth(r, h, 1, 0))
                if not (isinstance(r, int) and r == 0):
                    act.wait_ge(s_out[h], r * 16)
                nc.scalar.copy(y[:, h], ps[0:1, M3_BANK, 0:BLOCK].rearrange(
                    "p (s q) -> p q s", s=4)).then_inc(s_y, 1)
                act.wait_ge(s_y, nth(r, h, 1, 0))
                act.dma_start(out_v[r, h], y[:, h].rearrange("p q s -> p (q s)")).then_inc(s_out[h], 16)

            def unfold_out(r, h):
                for u in by_block(UNF_ACT, LAST_UNF_ACT, r, h):
                    act.wait_ge(s_unf, nth(r, h, NU, u))
                    unfold_group_out(copy, u).then_inc(s_unf_act, 1)

            def finish(r, h, between, first_tile):
                between(0, 2)
                unfold_out(r, h)
                between(2, 4)
                pairs_T_out(r, h)
                between(4, 5)
                (last_h1_out if is_last(r, h) else h1_out)(r, h)
                between(5, 6)
                h2_out(r, h)
                between(6, 7)
                first_tile()
                y_out(r, h)

            def turn(r):
                for h in range(2):
                    def selects(n0, n1):
                        for n in range(n0, n1):
                            select_out(r, h, n)

                    def groups(half):
                        for i in GROUPS_ACT:
                            act.wait_ge(s_tr, nth(r, h, 2 * NG, half * NG + i))
                            group_out(copy, 2 * h + half, i).then_inc(s_tr_act, 1)

                    def grams_moved(k0, k1):
                        for i, k in enumerate(by_block(GRAMS_ACT, LAST_GRAMS_ACT, r, h)):
                            if k0 <= k < k1:
                                act.wait_ge(s_gram, nth(r, h, GRAMS, k))
                                gram_out(act, copy, s_block_act, r, h, len(GRAMS_ACT), i, k, 0).then_inc(s_gram_act, 1)
                            if is_first(r, h) and k0 == 0 and k == 0:
                                split_pair_weights()
                            if k0 and k == 4:
                                dense_T_out()

                    if is_first(r, h):
                        selects(0, NS)
                        split_dense_weights()
                        groups(0)
                    else:
                        finish(r if h else r - 1, 1 - h, selects, lambda: groups(0))
                    grams_moved(0, 2)
                    groups(1)
                    grams_moved(2, GRAMS)
                    if is_first(r, h):
                        split_layer2_weights()

            turns(act, turn)
            finish(TURNS - 1, 1, lambda n0, n1: None, lambda: None)
            for h in range(2):
                act.wait_ge(s_out[h], 16 * TURNS)

        @block.vector
        def _(dve):
            def copy(dst, src):
                return nc.vector.tensor_copy(dst, src)

            def minus(lo, x, hi, landed):
                nc.vector.tensor_tensor(lo, x, hi.bitcast(fp32), ALU.subtract).then_inc(landed, 1)

            def split_pair_weights():
                for i, (_, n) in enumerate(K1):
                    dve.wait_ge(s_w_hi, 2 + i)
                    minus(w1p_lo[0:n, i], w1p[0:n, i], w1p_hi[0:n, i], s_w_lo)

            def split_layer2_weights():
                dve.wait_ge(s_w_hi, 2 + NK)
                minus(w2_lo[:, :, :], w2_raw, w2_hi[:, :, :], s_w_lo)

            def split_dense_weights():
                dve.wait_ge(s_w1d, 32)
                nc.vector.tensor_tensor(w1d[:, 0], w1d[:, 0], w1d[:, 1], ALU.add).then_inc(s_w_sum, 1)
                dve.wait_ge(s_w_hi, 1)
                minus(w1s_lo[:, :], w1d[:, 0], w1s_hi[:, :], s_w_lo)

            def dense_T_rest(r, h):
                dve.wait_ge(s_pt_hi, nth(r, h, NK + 1, 0))
                minus(dense_T_lo[:, :, :], dense_T[:, :, :], dense_T_hi[:, :, :], s_pt_lo)

            def pairs_T_rest(r, h):
                for k, (_, n) in enumerate(K1):
                    dve.wait_ge(s_pt_hi, nth(r, h, NK + 1, k + 1))
                    minus(pairs_T_lo[0:n, k], ps[0:n, PT_BANKS[k], 0:BLOCK].rearrange("p (s q) -> p s q", s=4),
                          pairs_T_hi[0:n, k], s_pt_lo)

            def h1_rest(r, h):
                for m in range(M1):
                    dve.wait_ge(s_h1, nth(r, h, M1, m))
                    minus(h1_lo[:, m], h1[:, m], h1_hi[:, m], s_h1_lo)

            def last_h1_rest(r, h):
                def rest(m):
                    dve.wait_ge(s_h1, nth(r, h, M1, m))
                    minus(h1_lo[:, m], h1[:, m], h1_hi[:, m], s_h1_lo)

                for m in range(M1):
                    dve.wait_ge(s_h1_hi, nth(r, h, M1, m))
                    nc.vector.tensor_scalar(h1[:, m, :], ps[:, LAST_M1_BANKS[m], 0:BLOCK], b1_sb[:, m:m + 1], 0.0,
                                            ALU.add, ALU.max).then_inc(s_h1, 1)
                    if m:
                        rest(m - 1)
                rest(M1 - 1)

            def split_table(n):
                dve.wait_ge(s_hi, n + 1)
                minus(table_lo[0:ROWS_P, n], raw[n][0:ROWS_P], table_hi[0:ROWS_P, n], s_lo)

            def make_onehot(r, h, n):
                if n == 0:
                    dve.wait_ge(s_ids_f, r * 2 + (h + 1))
                i = h * NS + n
                if not (isinstance(r, int) and r == 0 and i < 2):
                    dve.wait_ge(s_sel, r * (2 * NS) + (i - 1))
                for c in range(CHUNKS):
                    last = nc.vector.tensor_scalar(onehot[0:ROWS_P, i % 2, c, :], ids_f[0:ROWS_P, n, :],
                                                   float(c), None, ALU.is_equal)
                last.then_inc(s_onehot, 1)

            def ids_to_float(r, h):
                dve.wait_ge(s_ids_i, r * 32 + (16 * h + 16))
                nc.vector.tensor_scalar(ids_f[:, :, :], ids_i, first_row[:, 0:1], None, ALU.add).then_inc(s_ids_f, 1)

            def unfold_out(r, h):
                for u in by_block(UNF_DVE, LAST_UNF_DVE, r, h):
                    dve.wait_ge(s_unf, nth(r, h, NU, u))
                    unfold_group_out(copy, u).then_inc(s_unf_dve, 1)

            def turn(r):
                for h in range(2):
                    if is_first(r, h):
                        for n in range(NS):
                            split_table(n)
                            make_onehot(0, 0, n)
                        split_dense_weights()
                    else:
                        rb, hb = r if h else r - 1, 1 - h
                        make_onehot(r, h, 2)
                        make_onehot(r, h, 3)
                        unfold_out(rb, hb)
                        make_onehot(r, h, 4)
                        pairs_T_rest(rb, hb)
                        make_onehot(r, h, 5)
                        make_onehot(r, h, 6)
                        h1_rest(rb, hb)

                    def groups(half):
                        for i in GROUPS_DVE:
                            dve.wait_ge(s_tr, nth(r, h, 2 * NG, half * NG + i))
                            group_out(copy, 2 * h + half, i).then_inc(s_tr_dve, 1)

                    def grams_moved(k0, k1):
                        for i, k in enumerate(by_block(GRAMS_DVE, LAST_GRAMS_DVE, r, h)):
                            if k0 <= k < k1:
                                dve.wait_ge(s_gram, nth(r, h, GRAMS, k))
                                gram_out(dve, copy, s_block_dve, r, h, len(GRAMS_DVE), i, k, 1).then_inc(s_gram_dve, 1)
                            if k0 and k == 5:
                                dense_T_rest(r, h)

                    def build_ahead(*ns):
                        if not is_last(r, h):
                            ids_to_float(r + h, 1 - h)
                            for n in ns:
                                make_onehot(r + h, 1 - h, n)

                    groups(0)
                    grams_moved(0, GRAMS_AHEAD)
                    if is_first(r, h):
                        split_pair_weights()
                    groups(1)
                    build_ahead(0, 1)
                    grams_moved(GRAMS_AHEAD, GRAMS)
                    if is_first(r, h):
                        split_layer2_weights()

            turns(dve, turn)
            unfold_out(TURNS - 1, 1)
            pairs_T_rest(TURNS - 1, 1)
            last_h1_rest(TURNS - 1, 1)

        @block.tensor
        def _(pe):
            def select(r, h, n):
                i = h * NS + n
                pe.wait_ge(s_onehot, nth(r, h, NS, n))
                if not (isinstance(r, int) and r == 0 and i < 2):
                    pe.wait_ge(s_sel_out, r * (2 * NS) + (i - 1))
                for part in (table_hi, table_lo):
                    for c in range(CHUNKS):
                        last = nc.tensor.matmul(ps[:, SEL_BANKS[i % 2], 0:BLOCK], part[0:ROWS_P, n, c, :],
                                                onehot[0:ROWS_P, i % 2, c, :],
                                                start=part is table_hi and c == 0,
                                                stop=part is table_lo and c == CHUNKS - 1)
                last.then_inc(s_sel, 1)

            def wait_group_out(r, h, half, i):
                mine, moved = (GROUPS_ACT, s_tr_act) if i in GROUPS_ACT else (GROUPS_DVE, s_tr_dve)
                pe.wait_ge(moved, nth(r, h, 2 * len(mine), half * len(mine) + mine.index(i)))

            def transposes(r, h, half):
                t = 2 * h + half
                pe.wait_ge(s_dense[t], r * 16 + 16)
                slot = {0: 0}
                for j, f in enumerate(LARGE):
                    slot[1 + f] = 1 + j
                for i, (f0, step, cnt) in enumerate(GROUPS):
                    if i in PART_GROUPS:
                        part = PART_GROUPS.index(i)
                        pe.wait_ge(s_rows[t][part], r * (16 * PARTS[part]) + 16 * PARTS[part])
                    if half == 0 and i == 2:
                        pe.wait_ge(s_sel_out, nth(r, h, NS, NS - 1))
                    if i >= 4:
                        wait_group_out(r, h, half, i - 4)
                    for j in range(cnt):
                        last = nc.tensor.transpose(ps[:, TR_BANKS[i % 4], j * TILE:(j + 1) * TILE],
                                                   rows[:, t, slot[f0 + j * step], :], ident[:, :])
                    last.then_inc(s_tr, 1)

            def wait_gram_out(r, h, k):
                of_dve = by_block(GRAMS_DVE, LAST_GRAMS_DVE, r, h)
                of_act = by_block(GRAMS_ACT, LAST_GRAMS_ACT, r, h)
                if k in of_dve:
                    pe.wait_ge(s_gram_dve, nth(r, h, len(GRAMS_DVE), of_dve.index(k)))
                if k in of_act:
                    pe.wait_ge(s_gram_act, nth(r, h, len(GRAMS_ACT), of_act.index(k)))

            def wait_transposed(r, h, half):
                wait_group_out(r, h, half, GROUPS_DVE[-1])
                wait_group_out(r, h, half, GROUPS_ACT[-1])

            def gram(r, h, k0, k1):
                if k0 == 0:
                    pe.wait_ge(s_sel_out, nth(r, h, NS, NS - 1))
                    wait_transposed(r, h, 0)
                for k in range(k0, k1):
                    if k == 1 and not is_first(r, h):
                        pe.wait_ge(s_y, r * 2 + h)
                    if k == GRAMS // 2:
                        wait_transposed(r, h, 1)
                    if GRAM_BANKS[k] in GRAM_BANKS[:k]:
                        wait_gram_out(r, h, max(j for j in range(k) if GRAM_BANKS[j] == GRAM_BANKS[k]))
                    for b in range(2):
                        for j in range(QB):
                            s0 = 4 * (2 * QB * k + QB * b + j)
                            last = nc.tensor.matmul(
                                ps[0:QF, GRAM_BANKS[k] + b, j * 4 * COLS:(j + 1) * 4 * COLS],
                                X[:, s0:s0 + 4, :].rearrange("p b s -> p (b s)"),
                                X[:, s0:s0 + 4, 0:COLS], start=True, stop=True)
                    last.then_inc(s_gram, 1)

            def unfold(r, h):
                wait_gram_out(r, h, by_block(GRAMS_DVE, LAST_GRAMS_DVE, r, h)[-1])
                wait_gram_out(r, h, by_block(GRAMS_ACT, LAST_GRAMS_ACT, r, h)[-1])
                pe.sem_inc(s_pe_gate, 1)
                for u, fs in enumerate(UNF):
                    for j in range(0, len(fs), 2):
                        last = nc.tensor.transpose(
                            ps[:, UNF_BANKS[u], j // 2 * QF:(j // 2 + 1) * QF],
                            grams[0:QF, fs[j]:fs[j] + 2, :].rearrange("p f q -> p (f q)"), ident[0:QF, 0:QF])
                    last.then_inc(s_unf, 1)

            def pair_transposes(r, h):
                of_dve = by_block(UNF_DVE, LAST_UNF_DVE, r, h)
                of_act = by_block(UNF_ACT, LAST_UNF_ACT, r, h)
                pe.wait_ge(s_unf_dve, nth(r, h, len(UNF_DVE), len(of_dve) - 1))
                pe.wait_ge(s_unf_act, nth(r, h, len(UNF_ACT), len(of_act) - 1))
                pe.sem_inc(s_pe_gate, 1)
                for k, (k0, n) in enumerate(K1):
                    for s in range(4):
                        last = nc.tensor.transpose(ps[0:n, PT_BANKS[k], s * QUADS:(s + 1) * QUADS],
                                                   pairs[:, s, k0:k0 + n], ident[0:QUADS, 0:QUADS])
                    last.then_inc(s_pt, 1)

            def products(dst, w_hi, w_lo, x_hi, x_lo, start, stop):
                for w, x, s, e in ((w_hi, x_hi, start, False), (w_lo, x_hi, False, False), (w_hi, x_lo, False, stop)):
                    last = nc.tensor.matmul(dst, w, x, start=s, stop=e)
                return last

            def dense_products(m, bank):
                cols = slice(m * P, (m + 1) * P)
                products(ps[:, bank, 0:BLOCK], w1s_hi[:, cols], w1s_lo[:, cols],
                         dense_T_hi[:, :, :].rearrange("p s q -> p (s q)"),
                         dense_T_lo[:, :, :].rearrange("p s q -> p (s q)"), True, False)

            def pair_products(m, k, bank):
                n = K1[k][1]
                cols = slice(m * P, (m + 1) * P)
                last = products(ps[:, bank, 0:BLOCK], w1p_hi[0:n, k, cols], w1p_lo[0:n, k, cols],
                                pairs_T_hi[0:n, k].rearrange("p s q -> p (s q)"),
                                pairs_T_lo[0:n, k].rearrange("p s q -> p (s q)"), False, k == NK - 1)
                if k == NK - 1:
                    last.then_inc(s_m1, 1)

            def layer1(r, h):
                if is_first(r, h):
                    pe.wait_ge(s_w_lo, 2 + NK)
                    pe.wait_ge(s_bias, 48)
                pe.wait_ge(s_pt_lo, nth(r, h, NK + 1, NK))
                for m in range(M1):
                    dense_products(m, M1_BANKS[m])
                    for k in range(NK):
                        pair_products(m, k, M1_BANKS[m])

            def last_layer1(r, h):
                def product(m, k, w, x, stop=False):
                    n = K1[k][1]
                    return nc.tensor.matmul(ps[:, LAST_M1_BANKS[m], 0:BLOCK], w[0:n, k, m * P:(m + 1) * P],
                                            x[0:n, k].rearrange("p s q -> p (s q)"), start=False, stop=stop)

                for k in range(NK):
                    pe.wait_ge(s_pt_hi, nth(r, h, NK + 1, k + 1))
                    for m in range(M1):
                        product(m, k, w1p_hi, pairs_T_hi)
                pe.wait_ge(s_pt_lo, nth(r, h, NK + 1, NK))
                for m in range(M1):
                    for k in range(NK):
                        product(m, k, w1p_lo, pairs_T_hi)
                        last = product(m, k, w1p_hi, pairs_T_lo, k == NK - 1)
                    last.then_inc(s_m1, 1)

            def layer2(r, h):
                pe.wait_ge(s_h1_lo, nth(r, h, M1, M1 - 1))
                for m in range(M2):
                    cols = slice(m * P, (m + 1) * P)
                    for k in range(M1):
                        last = products(ps[:, M2_BANKS[m], 0:BLOCK], w2_hi[:, k, cols], w2_lo[:, k, cols],
                                        h1_hi[:, k], h1_lo[:, k], k == 0, k == M1 - 1)
                    last.then_inc(s_m2, 1)

            def last_layer2(r, h):
                def product(m, k, w, x, start=False, stop=False):
                    return nc.tensor.matmul(ps[:, M2_BANKS[m], 0:BLOCK], w[:, k, m * P:(m + 1) * P], x[:, k],
                                            start=start, stop=stop)

                for k in range(M1):
                    pe.wait_ge(s_h1_hi, nth(r, h, M1, k))
                    for m in range(M2):
                        product(m, k, w2_hi, h1_hi, start=k == 0)
                        product(m, k, w2_lo, h1_hi)
                pe.wait_ge(s_h1_lo, nth(r, h, M1, M1 - 1))
                for m in range(M2):
                    for k in range(M1):
                        last = product(m, k, w2_hi, h1_lo, stop=k == M1 - 1)
                    last.then_inc(s_m2, 1)

            def layer3(r, h):
                for k in range(M2):
                    pe.wait_ge(s_h2, nth(r, h, M2, k))
                    last = nc.tensor.matmul(ps[0:1, M3_BANK, 0:BLOCK], w3_sb[:, k:k + 1],
                                            h2[:, k, :], start=k == 0, stop=k == M2 - 1)
                last.then_inc(s_m3, 1)

            def finish(r, h, between, first_tile):
                between(0, 2)
                if is_last(r, h):
                    pe.wait_ge(s_pt_lo, nth(r, h, NK + 1, 0))
                    for m in (0, 1):
                        dense_products(m, LAST_M1_BANKS[m])
                unfold(r, h)
                if is_last(r, h):
                    for m in (2, 3):
                        dense_products(m, LAST_M1_BANKS[m])
                between(2, 4)
                pair_transposes(r, h)
                between(4, 5)
                (last_layer1 if is_last(r, h) else layer1)(r, h)
                between(5, 6)
                (last_layer2 if is_last(r, h) else layer2)(r, h)
                between(6, 7)
                first_tile()
                layer3(r, h)

            def turn(r):
                for h in range(2):
                    def selects(n0, n1):
                        for n in range(n0, n1):
                            if is_first(r, h):
                                pe.wait_ge(s_lo, n + 1)
                            select(r, h, n)

                    def first_tile():
                        transposes(r, h, 0)

                    if is_first(r, h):
                        selects(0, NS)
                        pe.wait_ge(s_const, 32)
                        first_tile()
                    else:
                        finish(r if h else r - 1, 1 - h, selects, first_tile)
                    ahead = GRAMS_AHEAD + int(is_first(r, h))
                    gram(r, h, 0, ahead)
                    transposes(r, h, 1)
                    gram(r, h, ahead, GRAMS)

            turns(pe, turn)
            finish(TURNS - 1, 1, lambda n0, n1: None, lambda: None)


_TABLES = [f"tbl_{i}" for i in range(FEATS - 1)]


def kernel(**inputs):
    import numpy as _np
    import concourse.bacc as _bacc
    from concourse import mybir as _mybir
    from concourse.bass_utils import run_bass_kernel_spmd as _run

    nc = _bacc.Bacc("TRN2", target_bir_lowering=False, num_devices=1)
    arrays = {}

    def dram(name, a):
        a = _np.ascontiguousarray(a)
        arrays[f"in_{name}"] = a
        return nc.dram_tensor(f"in_{name}", a.shape, _mybir.dt.from_np(a.dtype), kind="ExternalInput").ap()

    def columns(name, a):
        return dram(name, _np.asarray(a).reshape(-1, P).T)

    ids = _np.asarray(inputs["ids"])
    out = nc.dram_tensor("out", (BATCH, 1), _mybir.dt.float32, kind="ExternalOutput").ap()
    dlrm_kernel(
        nc, dram("dense", inputs["r_dense_features"]), dram("ids", ids),
        dram("ids_small", ids[:, SMALL].T), [dram(n, inputs[n]) for n in _TABLES],
        dram("w1", inputs["W_top1"]), columns("b1", inputs["b_top1"]), dram("w2", inputs["W_top2"]),
        columns("b2", inputs["b_top2"]), columns("w3", inputs["W_top3"]),
        dram("identity", _np.eye(P, dtype=_np.float32)),
        dram("minus_first_row", -CHUNKS * _np.arange(P, dtype=_np.float32).reshape(P, 1)), out)
    r = _run(nc, [arrays], core_ids=[0])
    return r.results[0]["out"]
```
